# Optimizing a Trainium2 kernel written in Bass

```python
import numpy as np
import jax
import jax.numpy as jnp

def _softmax(x, axis=-1):
    return jax.nn.softmax(x, axis=axis)

def _gelu(x):
    return jax.nn.gelu(x, approximate=True)

def _silu(x):
    return jax.nn.silu(x)

def _sigmoid(x):
    return jax.nn.sigmoid(x)

def _layernorm(x, axis=-1, eps=1e-05):
    m = jnp.mean(x, axis=axis, keepdims=True)
    v = jnp.var(x, axis=axis, keepdims=True)
    return (x - m) / jnp.sqrt(v + eps)

def _scatter_add(tgt, idx, src, axis=0):
    return tgt.at[idx].add(src)

def _segment_sum(src, seg, n):
    return jax.ops.segment_sum(src, seg, n)
kernel_name = 'mk_flamingo_gated_d1_seqx_r8_aa400f'

def setup_inputs(seed: int=0):
    np.random.seed(seed)
    _w = jnp.asarray

    def _rec_inputs():
        import jax
        import jax.numpy as jnp
        _rk = jax.random.key(seed)
        x = 4.136e-05 + 0.9999 * jax.random.normal(jax.random.fold_in(_rk, 1), (4, 512, 128), jnp.float32)
        _lenS = 512 - jax.random.randint(jax.random.fold_in(_rk, 7), (4,), 0, max(1, 512 // 4) + 1, jnp.int32)
        _lenS2 = 32 - jax.random.randint(jax.random.fold_in(_rk, 8), (4,), 0, max(1, 32 // 4) + 1, jnp.int32)
        _ctx_2048P = jax.random.normal(jax.random.fold_in(_rk, 11), (4, 16, 256), jnp.float32)
        _ctx_2048c = jax.random.dirichlet(jax.random.fold_in(_rk, 511), 0.3 * jnp.ones((16,), jnp.float32), (4, 32))
        _ctx_2048t = jnp.einsum('bsk,bkd->bsd', _ctx_2048c, _ctx_2048P)
        _ctx_2048t = _ctx_2048t * jax.lax.rsqrt(jnp.mean(jnp.square(_ctx_2048t)) + 1e-12) * 0.953939
        ctx_2048 = -0.000392918 + 0.999932 * (_ctx_2048t + 0.3 * jax.random.normal(jax.random.fold_in(_rk, 611), (4, 32, 256), jnp.float32))
        _validS = jnp.arange(512)[None, :] < _lenS[:, None]
        _validS2 = jnp.arange(32)[None, :] < _lenS2[:, None]
        _causal = jnp.tril(jnp.ones((512, 512), dtype=bool))
        mask_BxS2_ik0 = jnp.where(jnp.broadcast_to(_validS2[:, :], (4, 32)), 0, 1).astype(jnp.int32)
        _g = jax.random.normal(jax.random.fold_in(_rk, 9001), (2, 1), jnp.float32)
        _g = jnp.sign(_g) * jnp.maximum(jnp.abs(_g), 1.0) + (_g == 0) * 1.0
        g_xattn = _g[0]
        g_ffn = _g[1]
        return (x, ctx_2048, mask_BxS2_ik0, g_xattn, g_ffn)
    x, ctx_2048, mask_BxS2_ik0, g_xattn, g_ffn = _rec_inputs()

    def _L0_xattn_setup():
        import jax, jax.numpy as jnp
        import numpy as np
        UNITS = 128
        NUM_HEADS = 8

        def _split_heads(x, n):
            B, S, D = x.shape
            return x.reshape(B, S, n, D // n).transpose(0, 2, 1, 3)
        key = jax.random.key(seed)
        k1, k2, k3 = jax.random.split(key, 3)
        B, S = (8, 128)
        memory = jax.random.normal(k1, (B, S, 2 * UNITS), dtype=jnp.float32)
        query = jax.random.normal(k2, (B, S, UNITS), dtype=jnp.float32)
        seq_mask = jax.random.randint(k3, (B, S), 0, 2, dtype=jnp.int32)
        b = jnp.zeros((1,), dtype=jnp.float32)
        return {'memory': memory, 'query': query, 'seq_mask': seq_mask, 'b': b}
    _L0_xattn_all = _L0_xattn_setup()
    _L0_xattn_in = {k: v for k, v in _L0_xattn_all.items() if k in ('b',)}
    del _L0_xattn_all

    def _L0_ffn_setup():
        import jax, jax.numpy as jnp
        import numpy as np
        DIM = 128
        DEPTH = 6
        HEADS = 16
        DIM_HEAD = 64
        WINDOW = 32
        INNER = HEADS * DIM_HEAD
        DIM_INNER = int(DIM * 4 * 2 / 3)
        QK_SCALE = 8.0

        def shift_tokens(t):
            a, s = jnp.split(t, 2, -1)
            s = jnp.pad(s, ((0, 0), (1, 0), (0, 0)))[:, :-1]
            return jnp.concatenate([a, s], -1)

        def l2norm(t):
            return t / jnp.maximum(jnp.linalg.norm(t, axis=-1, keepdims=True), 1e-12)

        def rotate_half(x):
            x1, x2 = jnp.split(x, 2, -1)
            return jnp.concatenate([-x2, x1], -1)

        def rotary_tables(n):
            half = jnp.arange(0, DIM_HEAD, 2, dtype=jnp.float32)
            inv_freq = 1.0 / 10000.0 ** (half / DIM_HEAD)
            t = jnp.arange(n, dtype=jnp.float32)
            freqs = t[:, None] * inv_freq[None, :]
            freqs = jnp.concatenate([freqs, freqs], -1)
            base_scale = (half + 0.4 * DIM_HEAD) / (1.4 * DIM_HEAD)
            power = (t - n // 2) / (WINDOW // 2)
            scale = base_scale[None, :] ** power[:, None]
            scale = jnp.concatenate([scale, scale], -1)
            return (freqs, scale)

        def local_attention(q, k, v):
            b, h, n, d = q.shape
            w = WINDOW
            nw = n // w
            bq = q.reshape(b, h, nw, w, d)
            bk = k.reshape(b, h, nw, w, d)
            bv = v.reshape(b, h, nw, w, d)

            def look(t):
                p = jnp.pad(t, ((0, 0), (0, 0), (1, 0), (0, 0), (0, 0)))
                return jnp.concatenate([p[:, :, :nw], p[:, :, 1:]], axis=3)
            bk2, bv2 = (look(bk), look(bv))
            seq = jnp.arange(n).reshape(nw, w)
            seq_p = jnp.pad(seq, ((1, 0), (0, 0)), constant_values=-1)
            jt = jnp.concatenate([seq_p[:nw], seq_p[1:]], axis=1)
            it = seq[:, :, None]
            jb = jt[:, None, :]
            mask = (it < jb) | (it > jb + w) | (jb == -1)
            sim = jnp.einsum('bhwie,bhwje->bhwij', bq, bk2) * QK_SCALE
            sim = jnp.where(mask, -jnp.finfo(sim.dtype).max, sim)
            attn = jax.nn.softmax(sim, -1)
            out = jnp.einsum('bhwij,bhwje->bhwie', attn, bv2)
            return out.reshape(b, h, n, d)

        def attn_layer(x, Wqkv, qs, ksc, Wo):
            b, n, _ = x.shape
            qkv = x @ Wqkv
            q, k, v = jnp.split(qkv, 3, -1)
            sh = lambda t: t.reshape(b, n, HEADS, DIM_HEAD).transpose(0, 2, 1, 3)
            q, k, v = (sh(q), sh(k), sh(v))
            q = l2norm(q) * qs
            k = l2norm(k) * ksc
            freqs, scale = rotary_tables(n)
            cos, sin = (jnp.cos(freqs), jnp.sin(freqs))
            q = q * cos * scale + rotate_half(q) * sin * scale
            inv = 1.0 / scale
            k = k * cos * inv + rotate_half(k) * sin * inv
            out = local_attention(q, k, v)
            out = out.transpose(0, 2, 1, 3).reshape(b, n, INNER)
            return out @ Wo

        def ffn_layer(x, g, bln, W1, b1, W2, b2):
            mu = x.mean(-1, keepdims=True)
            var = ((x - mu) ** 2).mean(-1, keepdims=True)
            xn = (x - mu) / jnp.sqrt(var + 1e-05) * g + bln
            hg = xn @ W1 + b1
            a, gate = jnp.split(hg, 2, -1)
            return a * jax.nn.gelu(gate, approximate=False) @ W2 + b2
        key = jax.random.key(seed)
        ks = jax.random.split(key, 8)
        B, N = (2, 256)
        init = lambda k, shape: jax.random.normal(k, shape, jnp.float32) * 0.02
        return {'x': jax.random.normal(ks[0], (B, N, DIM), jnp.float32), 'Wqkv': init(ks[1], (DEPTH, DIM, 3 * INNER)), 'q_scale': jnp.ones((DEPTH, DIM_HEAD), jnp.float32), 'k_scale': jnp.ones((DEPTH, DIM_HEAD), jnp.float32), 'Wo': init(ks[2], (DEPTH, INNER, DIM)), 'ln_g': jnp.ones((DEPTH, DIM), jnp.float32), 'ln_b': jnp.zeros((DEPTH, DIM), jnp.float32), 'W1': init(ks[3], (DEPTH, DIM, 2 * DIM_INNER)), 'b1': jnp.zeros((DEPTH, 2 * DIM_INNER), jnp.float32), 'W2': init(ks[4], (DEPTH, DIM_INNER, DIM)), 'b2': jnp.zeros((DEPTH, DIM), jnp.float32)}
    _L0_ffn_all = _L0_ffn_setup()
    _L0_ffn_in = {k: v for k, v in _L0_ffn_all.items() if k in ('Wqkv', 'q_scale', 'k_scale', 'Wo', 'ln_g', 'ln_b', 'W1', 'b1', 'W2', 'b2')}
    del _L0_ffn_all
    return {'x': x, 'ctx_2048': ctx_2048, 'mask_BxS2_ik0': mask_BxS2_ik0, 'g_xattn': g_xattn, 'g_ffn': g_ffn, 'L0_xattn_b': _L0_xattn_in['b'], 'L0_ffn_Wqkv': _L0_ffn_in['Wqkv'], 'L0_ffn_q_scale': _L0_ffn_in['q_scale'], 'L0_ffn_k_scale': _L0_ffn_in['k_scale'], 'L0_ffn_Wo': _L0_ffn_in['Wo'], 'L0_ffn_ln_g': _L0_ffn_in['ln_g'], 'L0_ffn_ln_b': _L0_ffn_in['ln_b'], 'L0_ffn_W1': _L0_ffn_in['W1'], 'L0_ffn_b1': _L0_ffn_in['b1'], 'L0_ffn_W2': _L0_ffn_in['W2'], 'L0_ffn_b2': _L0_ffn_in['b2']}

def reference(x, ctx_2048, mask_BxS2_ik0, g_xattn, g_ffn, L0_xattn_b, L0_ffn_Wqkv, L0_ffn_q_scale, L0_ffn_k_scale, L0_ffn_Wo, L0_ffn_ln_g, L0_ffn_ln_b, L0_ffn_W1, L0_ffn_b1, L0_ffn_W2, L0_ffn_b2):
    import jax
    import jax.numpy as jnp

    def _L0_xattn_ref(memory, query, seq_mask, b):
        import jax, jax.numpy as jnp
        import numpy as np
        UNITS = 128
        NUM_HEADS = 8

        def _split_heads(x, n):
            B, S, D = x.shape
            return x.reshape(B, S, n, D // n).transpose(0, 2, 1, 3)
        H = NUM_HEADS
        depth = UNITS // H
        Q = _split_heads(query, H) * depth ** (-0.5)
        k_mem, v_mem = jnp.split(memory, 2, axis=2)
        K = _split_heads(k_mem, H)
        V = _split_heads(v_mem, H)
        logits = jnp.einsum('bhqd,bhkd->bhqk', Q, K) + b[0]
        mask = seq_mask.astype(jnp.float32)[:, None, None, :]
        logits = logits + -1e+30 * (1.0 - mask)
        weights = jax.nn.softmax(logits, axis=-1)
        out = jnp.einsum('bhqk,bhkd->bhqd', weights, V)
        B, _, S, _ = out.shape
        return out.transpose(0, 2, 1, 3).reshape(B, S, UNITS)

    def _L0_ffn_ref(x, Wqkv, q_scale, k_scale, Wo, ln_g, ln_b, W1, b1, W2, b2):
        import jax, jax.numpy as jnp
        import numpy as np
        DIM = 128
        DEPTH = 6
        HEADS = 16
        DIM_HEAD = 64
        WINDOW = 32
        INNER = HEADS * DIM_HEAD
        DIM_INNER = int(DIM * 4 * 2 / 3)
        QK_SCALE = 8.0

        def shift_tokens(t):
            a, s = jnp.split(t, 2, -1)
            s = jnp.pad(s, ((0, 0), (1, 0), (0, 0)))[:, :-1]
            return jnp.concatenate([a, s], -1)

        def l2norm(t):
            return t / jnp.maximum(jnp.linalg.norm(t, axis=-1, keepdims=True), 1e-12)

        def rotate_half(x):
            x1, x2 = jnp.split(x, 2, -1)
            return jnp.concatenate([-x2, x1], -1)

        def rotary_tables(n):
            half = jnp.arange(0, DIM_HEAD, 2, dtype=jnp.float32)
            inv_freq = 1.0 / 10000.0 ** (half / DIM_HEAD)
            t = jnp.arange(n, dtype=jnp.float32)
            freqs = t[:, None] * inv_freq[None, :]
            freqs = jnp.concatenate([freqs, freqs], -1)
            base_scale = (half + 0.4 * DIM_HEAD) / (1.4 * DIM_HEAD)
            power = (t - n // 2) / (WINDOW // 2)
            scale = base_scale[None, :] ** power[:, None]
            scale = jnp.concatenate([scale, scale], -1)
            return (freqs, scale)

        def local_attention(q, k, v):
            b, h, n, d = q.shape
            w = WINDOW
            nw = n // w
            bq = q.reshape(b, h, nw, w, d)
            bk = k.reshape(b, h, nw, w, d)
            bv = v.reshape(b, h, nw, w, d)

            def look(t):
                p = jnp.pad(t, ((0, 0), (0, 0), (1, 0), (0, 0), (0, 0)))
                return jnp.concatenate([p[:, :, :nw], p[:, :, 1:]], axis=3)
            bk2, bv2 = (look(bk), look(bv))
            seq = jnp.arange(n).reshape(nw, w)
            seq_p = jnp.pad(seq, ((1, 0), (0, 0)), constant_values=-1)
            jt = jnp.concatenate([seq_p[:nw], seq_p[1:]], axis=1)
            it = seq[:, :, None]
            jb = jt[:, None, :]
            mask = (it < jb) | (it > jb + w) | (jb == -1)
            sim = jnp.einsum('bhwie,bhwje->bhwij', bq, bk2) * QK_SCALE
            sim = jnp.where(mask, -jnp.finfo(sim.dtype).max, sim)
            attn = jax.nn.softmax(sim, -1)
            out = jnp.einsum('bhwij,bhwje->bhwie', attn, bv2)
            return out.reshape(b, h, n, d)

        def attn_layer(x, Wqkv, qs, ksc, Wo):
            b, n, _ = x.shape
            qkv = x @ Wqkv
            q, k, v = jnp.split(qkv, 3, -1)
            sh = lambda t: t.reshape(b, n, HEADS, DIM_HEAD).transpose(0, 2, 1, 3)
            q, k, v = (sh(q), sh(k), sh(v))
            q = l2norm(q) * qs
            k = l2norm(k) * ksc
            freqs, scale = rotary_tables(n)
            cos, sin = (jnp.cos(freqs), jnp.sin(freqs))
            q = q * cos * scale + rotate_half(q) * sin * scale
            inv = 1.0 / scale
            k = k * cos * inv + rotate_half(k) * sin * inv
            out = local_attention(q, k, v)
            out = out.transpose(0, 2, 1, 3).reshape(b, n, INNER)
            return out @ Wo

        def ffn_layer(x, g, bln, W1, b1, W2, b2):
            mu = x.mean(-1, keepdims=True)
            var = ((x - mu) ** 2).mean(-1, keepdims=True)
            xn = (x - mu) / jnp.sqrt(var + 1e-05) * g + bln
            hg = xn @ W1 + b1
            a, gate = jnp.split(hg, 2, -1)
            return a * jax.nn.gelu(gate, approximate=False) @ W2 + b2
        for i in range(DEPTH):
            x = attn_layer(shift_tokens(x), Wqkv[i], q_scale[i], k_scale[i], Wo[i]) + x
            x = ffn_layer(shift_tokens(x), ln_g[i], ln_b[i], W1[i], b1[i], W2[i], b2[i]) + x
        return x
    x = x + jnp.tanh(g_xattn[0]) * _L0_xattn_ref(ctx_2048, _layernorm(x, axis=-1), mask_BxS2_ik0, L0_xattn_b)
    x = x + jnp.tanh(g_ffn[0]) * _L0_ffn_ref(_layernorm(x, axis=-1), L0_ffn_Wqkv, L0_ffn_q_scale, L0_ffn_k_scale, L0_ffn_Wo, L0_ffn_ln_g, L0_ffn_ln_b, L0_ffn_W1, L0_ffn_b1, L0_ffn_W2, L0_ffn_b2)
    return x

_drawn_inputs = setup_inputs


def setup_inputs(seed=0):
    import zlib

    import numpy as np

    out = dict(_drawn_inputs(seed))
    spreads = {'L0_ffn_q_scale': (1.0, 0.544),
     'L0_ffn_k_scale': (1.0, 0.6),
     'L0_ffn_ln_g': (1.0, 0.6),
     'L0_ffn_ln_b': (0.0, 0.8),
     'L0_ffn_b1': (0.0, 0.1),
     'L0_ffn_b2': (0.0, 0.1)}
    factors = {}
    for name, (base, spread) in spreads.items():
        noise = np.random.default_rng([zlib.crc32(name.encode()), seed]).standard_normal(out[name].shape)
        drawn = base * np.exp(spread * noise) if base else spread * noise
        out[name] = jnp.asarray(drawn.astype(out[name].dtype))
    for name, factor in factors.items():
        out[name] = (out[name] * factor).astype(out[name].dtype)
    return out
```

```python
from contextlib import ExitStack

import numpy as np

import concourse.bass as bass
from concourse import mybir

F32 = mybir.dt.float32
BF16 = mybir.dt.bfloat16
I32 = mybir.dt.int32
ALU = mybir.AluOpType
ACT = mybir.ActivationFunctionType
AX = mybir.AxisListType.X

P = 128
BATCHES, TOKENS, DIM = 4, 512, 128
DEPTH, HEADS, DHEAD, WINDOW = 6, 16, 64, 32
HALF = DHEAD // 2
INNER = HEADS * DHEAD
HIDDEN = int(DIM * 4 * 2 / 3)
QK_SCALE = 8.0
NORM_FLOOR = 1e-12
LN_EPS = 1e-5
BLOCKS = TOKENS // P
SLOTS = 4
PAIRS = HEADS // 2
QT = 64
KT = QT + WINDOW
TURNS = DEPTH * BATCHES
PER_TURN = BLOCKS * SLOTS
HID_PARTS = (114, 114, 113)
HID_MAX = 114
MASKED = -float(2 ** 100)
XHEADS, XKEYS = 8, 32
XDEPTH = DIM // XHEADS
XSCALE = float(XDEPTH) ** -0.5

C_IDENT = 0
C_BAND = C_IDENT + P
C_HEADK = C_BAND + 2 * KT
C_HEADV = C_HEADK + XHEADS
C_COS_Q = C_HEADV + 2 * P
C_SIN_Q = C_COS_Q + BLOCKS * DHEAD
C_COS_K = C_SIN_Q + BLOCKS * DHEAD
C_SIN_K = C_COS_K + BLOCKS * DHEAD
C_END = C_SIN_K + BLOCKS * DHEAD


def shape_constants():
    c = np.zeros((P, C_END), np.float32)
    row = np.arange(P)[:, None]
    c[:, C_IDENT:C_IDENT + P] = np.eye(P)
    key = np.arange(KT)[None, :]
    query = row % QT
    seen = (key >= query) & (key <= query + WINDOW)
    c[:, C_BAND:C_BAND + KT] = np.where(seen & (key >= WINDOW), 0.0, MASKED)
    c[:, C_BAND + KT:C_BAND + 2 * KT] = np.where(seen, 0.0, MASKED)
    c[:, C_HEADK:C_HEADK + XHEADS] = row // XDEPTH == np.arange(XHEADS)[None, :]
    for j in range(2):
        c[:, C_HEADV + j * P:C_HEADV + (j + 1) * P] = row // XKEYS + 4 * j == np.arange(P)[None, :] // XDEPTH
    half = np.arange(0, DHEAD, 2, dtype=np.float32)
    inv_freq = (1.0 / 10000.0 ** (half.astype(np.float64) / DHEAD)).astype(np.float32)
    t = np.arange(TOKENS, dtype=np.float32)
    freqs = (t[:, None] * inv_freq[None, :]).astype(np.float32).astype(np.float64)
    base = (half.astype(np.float64) + 0.4 * DHEAD) / (1.4 * DHEAD)
    power = (t.astype(np.float64) - TOKENS // 2) / (WINDOW // 2)
    scale = base[None, :] ** power[:, None]
    sign = np.concatenate([-np.ones(HALF), np.ones(HALF)])
    for at_cos, at_sin, s in ((C_COS_Q, C_SIN_Q, scale), (C_COS_K, C_SIN_K, 1.0 / scale)):
        cos = np.tile(np.cos(freqs) * s, 2)
        sin = np.tile(np.sin(freqs) * s, 2) * sign
        for at, table in ((at_cos, cos), (at_sin, sin)):
            c[:, at:at + BLOCKS * DHEAD] = table.reshape(BLOCKS, P, DHEAD).transpose(1, 0, 2).reshape(P, -1)
    return c


def build(nc, x, ctx_mem, mask, g_xattn, g_ffn, xb, wqkv, q_scale, k_scale, wo, ln_g, ln_b, w1, b1, w2, b2,
          consts, out):
    ctx = ExitStack()
    with ctx:
        def sb(name, shape, dt=F32):
            return ctx.enter_context(nc.sbuf_tensor(name, shape, dt))

        def sem(name):
            return ctx.enter_context(nc.semaphore(name))

        const = sb("const", [P, C_END])
        ident = const[:, C_IDENT:C_IDENT + P]
        ident_bf = sb("ident_bf", [P, P], BF16)
        band_bf = sb("band_bf", [P, 2, KT], BF16)
        mean_w = sb("mean_w", [P, P])
        ln_eps = sb("ln_eps", [P, 1])
        minus_half = sb("minus_half", [P, 8])
        gates = sb("gates", [P, 2])
        tanh_gates = sb("tanh_gates", [P, 2])
        x_tok = sb("x_tok", [P, BATCHES * BLOCKS, DIM])
        stream = sb("stream", [P, BATCHES, TOKENS])
        wqkv_sb = sb("wqkv_sb", [P, 2, 3 * INNER])
        wo_sb = sb("wo_sb", [P, PAIRS, DIM])
        w1_sb = sb("w1_sb", [P, 2 * HIDDEN])
        w2_sb = sb("w2_sb", [HID_MAX, 3, DIM])
        ln_g_sb = sb("ln_g_sb", [P, 1])
        ln_b_sb = sb("ln_b_sb", [P, 1])
        b2_sb = sb("b2_sb", [P, 1])
        b1_sb = sb("b1_sb", [HID_MAX, 2, 3])
        head_scales = sb("head_scales", [P, 4, DEPTH, DHEAD])
        rot = sb("rot", [P, 2, 4, BLOCKS, DHEAD])
        shifted = sb("shifted", [P, WINDOW + TOKENS])
        squares = sb("squares", [P, 2, 512])
        norm2 = sb("norm2", [P, 4, 8])
        norm2_floored = sb("norm2_floored", [P, 4, 8])
        inv_norm = sb("inv_norm", [P, 4, 8])
        normed = sb("normed", [P, 2, 512])
        sin_part = sb("sin_part", [P, 2, 512])
        rotated = sb("rotated", [P, 8, 512])
        q_diag = sb("q_diag", [P, 2, 2, PAIRS, P])
        k_T = sb("k_T", [P, PAIRS, WINDOW + TOKENS])
        v_tile = sb("v_tile", [KT, 2 * BLOCKS, INNER])
        row_max = sb("row_max", [P, 2, 4])
        neg_max = sb("neg_max", [P, 2, 4])
        row_sum = sb("row_sum", [P, 2, 4])
        inv_sum = sb("inv_sum", [P, 2, 4])
        probs = sb("probs", [P, 2, 4, KT])
        probs_T = sb("probs_T", [KT, 2, 4, P])
        attn_T = sb("attn_T", [P, PAIRS, TOKENS])
        mid = sb("mid", [P, TOKENS])
        ff_in = sb("ff_in", [P, TOKENS])
        ff_std = sb("ff_std", [P, TOKENS])
        ff_norm = sb("ff_norm", [P, TOKENS])
        gate_sb = sb("gate_sb", [HID_MAX, 3, TOKENS])

        ps = ctx.enter_context(nc.psum_tensor("ps", [P, 8, 512], F32))
        PS_V, PS_QKT, PS_S, PS_PT, PS_O, PS_FF = 2, 3, 4, 5, 6, 7

        const_in, x_in, ctx_in, small_in, scales_in = (sem(n) for n in ("const_in", "x_in", "ctx_in", "small_in",
                                                                        "scales_in"))
        wqkv_in, wo_in, ff_w_in, out_stored = (sem(n) for n in ("wqkv_in", "wo_in", "ff_w_in", "out_stored"))
        setup_dve, setup_pool = sem("setup_dve"), sem("setup_pool")
        head_dve, head_act, head_pe = sem("head_dve"), sem("head_act"), sem("head_pe")
        tail_pe, tail_dve = sem("tail_pe"), sem("tail_dve")
        tables_ready, shifted_ready = sem("tables_ready"), sem("shifted_ready")
        proj_ready, v_ready, qkT_ready, s_ready, pT_ready, o_ready = (
            sem(n) for n in ("proj_ready", "v_ready", "qkT_ready", "s_ready", "pT_ready", "o_ready"))
        squares_ready, norm2_ready, floored_ready, inv_norm_ready, normed_ready = (
            sem(n) for n in ("squares_ready", "norm2_ready", "floored_ready", "inv_norm_ready", "normed_ready"))
        cos_ready, sin_ready, rotated_ready = sem("cos_ready"), sem("sin_ready"), sem("rotated_ready")
        q_top_ready, q_low_ready, k_ready, v_kept = (
            sem(n) for n in ("q_top_ready", "q_low_ready", "k_ready", "v_kept"))
        max_ready, neg_max_ready, exp_ready, inv_sum_ready, probs_ready, pT_kept = (
            sem(n) for n in ("max_ready", "neg_max_ready", "exp_ready", "inv_sum_ready", "probs_ready", "pT_kept"))
        o_top_kept, o_low_kept = sem("o_top_kept"), sem("o_low_kept")
        wo_ready, mean_ready, var_ready, gate_ready, lin_ready, w2_ready = (
            sem(n) for n in ("wo_ready", "mean_ready", "var_ready", "gate_ready", "lin_ready", "w2_ready"))
        mid_ready, ff_in_ready, centred, ff_sq_ready, std_ready, ff_dve = (
            sem(n) for n in ("mid_ready", "ff_in_ready", "centred", "ff_sq_ready", "std_ready", "ff_dve"))
        ff_norm_ready, gate_kept, gelu_ready, hidden_ready, stream_ready = (
            sem(n) for n in ("ff_norm_ready", "gate_kept", "gelu_ready", "hidden_ready", "stream_ready"))

        def after(eng, s, value):
            if not isinstance(value, int) or value > 0:
                eng.wait_ge(s, value)

        def turns(eng, slot):
            def turn(it, nominal):
                for u in range(BLOCKS):
                    for s in range(SLOTS):
                        slot(it, nominal, u, s)
            turn(0, 0)
            turn(1, 1)
            with eng.Fori(2, TURNS - 1) as it:
                turn(it, 2)
            for last in range(TURNS - 1, TURNS + 3):
                turn(last, last)

        def in_body(nominal, u, s, lag):
            return 0 <= PER_TURN * nominal + SLOTS * u + s - lag < PER_TURN * TURNS

        def ff_turn(it, nominal, lag):
            return it - lag if 0 <= nominal - lag < TURNS else None

        def pick(tensor, index):
            if isinstance(index, int):
                return tensor[:, index, :]
            return tensor[:, bass.ds(index, 1), :].rearrange("p a n -> p (a n)")

        spare = attn_T[:, :, :].rearrange("p j t -> p (j t)")
        places = iter(np.cumsum([0, 512, 512, 128, 128, 1024, 1024]).tolist())

        def part(at, count, n):
            return spare[:, at:at + count * n].rearrange("p (a n) -> p a n", n=n)

        ctx_k = part(next(places), BATCHES, DIM)[0:XKEYS]
        ctx_v = part(next(places), BATCHES, DIM)
        mask_i = part(next(places), 1, BATCHES * XKEYS).rearrange("p a n -> p (a n)").bitcast(I32)
        logit_bias = part(next(places), BATCHES, XKEYS)
        key_diag = part(next(places), BATCHES, XHEADS * XKEYS)
        value_diag = part(next(places), 2 * BATCHES, DIM)
        xbias = sb("xbias", [P, 1])
        h_stat = sb("h_stat", [P, 8, BLOCKS])
        h_x = q_diag[:, 0, 0, 0:4, :]
        h_sq = q_diag[:, 0, 0, 4:8, :]
        h_T = q_diag[:, 0, 1, 0:4, :]
        h_logit = q_diag[:, 1, :, :, :].rearrange("p a b c -> p (a b c)")[:, 0:1024]
        h_exp = q_diag[:, 1, :, :, :].rearrange("p a b c -> p (a b c)")[:, 1024:2048]
        h_expT = rotated[:, 0:2, :].rearrange("p a b -> p (a b)")
        h_red = rotated[:, 2, 0:32]
        h_inv = rotated[:, 2, 32:64]

        def keep_q(copy, side, cs, cu):
            src = ps[side * QT:(side + 1) * QT, PS_QKT, :].rearrange("p (j t q) -> p j t q", j=4, t=2)
            dst = q_diag[side * QT:(side + 1) * QT, cu % 2, :, 4 * cs:4 * cs + 4, side * QT:(side + 1) * QT]
            return copy(dst.rearrange("p t j q -> p j t q"), src)

        def keep_o(eng, copy, side, u, s):
            g = (SLOTS * u + s - 11) % PER_TURN
            tile, half = g // 2, g % 2
            src = ps[side * QT:(side + 1) * QT, PS_O, :].rearrange("p (j x q) -> p j x q", j=4, x=2)[:, :, side, :]
            return copy(attn_T[side * QT:(side + 1) * QT, 4 * half:4 * half + 4, QT * tile:QT * (tile + 1)], src)

        block = ctx.enter_context(nc.Block())

        FF_LOADS = 16 * (1 + 3 * len(HID_PARTS) + 3)

        @block.sync
        def _(sp):
            sp.dma_start(const[:, :], consts).then_inc(const_in, 16)
            sp.dma_start(x_tok[:, :, :], x.rearrange("b (t p) c -> p (b t) c", p=P)).then_inc(x_in, 16)
            sp.dma_start(ctx_k[:, :, :], ctx_mem[:, :, 0:DIM].rearrange("b k c -> k b c")).then_inc(ctx_in, 16)
            for quad in range(4):
                sp.dma_start(ctx_v[quad * XKEYS:(quad + 1) * XKEYS, :, :],
                             ctx_mem[:, :, DIM:2 * DIM].rearrange("b k c -> k b c")).then_inc(ctx_in, 16)
            sp.dma_start(mask_i[:, :], mask.rearrange("(o b) k -> o (b k)", o=1).to_broadcast([P, BATCHES * XKEYS])
                         ).then_inc(small_in, 16)
            for dst, src in ((xbias[:, :], xb), (gates[:, 0:1], g_xattn), (gates[:, 1:2], g_ffn)):
                sp.dma_start(dst, src.rearrange("(o n) -> o n", o=1).to_broadcast([P, 1])).then_inc(small_in, 16)
            for n, src in ((0, q_scale), (2, k_scale)):
                s3 = src.rearrange("(o l) d -> o l d", o=1)
                sp.dma_start(head_scales[:, n, :, :], s3.to_broadcast([P, DEPTH, DHEAD])).then_inc(scales_in, 16)
                for h in range(2):
                    sp.dma_start(head_scales[:, n + 1, :, h * HALF:(h + 1) * HALF],
                                 s3[:, :, (1 - h) * HALF:(2 - h) * HALF].to_broadcast([P, DEPTH, HALF])
                                 ).then_inc(scales_in, 16)

            def load_wqkv(place, row):
                sp.dma_start(pick(wqkv_sb, place), rows(wqkv, row, DIM)).then_inc(wqkv_in, 16)

            def rows(t, at, n):
                return t[at:at + n, :] if isinstance(at, int) else t[bass.ds(at, n), :]

            def load_wo(layer):
                sp.dma_start(wo_sb[:, :, :], rows(wo, layer * INNER, INNER).rearrange("(j p) c -> p j c", p=P)
                             ).then_inc(wo_in, 16)

            def load_ff(layer):
                sp.dma_start(w1_sb[:, :], rows(w1, layer * DIM, DIM)).then_inc(ff_w_in, 16)
                at = 0
                for j, m in enumerate(HID_PARTS):
                    sp.dma_start(w2_sb[0:m, j, :], rows(w2, layer * HIDDEN + at, m)).then_inc(ff_w_in, 16)
                    for part in range(2):
                        sp.dma_start(b1_sb[0:m, part, j:j + 1], rows(b1, layer * 2 * HIDDEN + part * HIDDEN + at, m)
                                     ).then_inc(ff_w_in, 16)
                    at += m
                for dst, src in ((ln_g_sb, ln_g), (ln_b_sb, ln_b), (b2_sb, b2)):
                    sp.dma_start(dst[:, :], rows(src, layer * DIM, DIM)).then_inc(ff_w_in, 16)

            load_wqkv(0, 0)
            load_wo(0)
            load_ff(0)
            sp.wait_ge(wqkv_in, 16)
            load_wqkv(1, DIM)

            def next_layer(layer, wqkv_too):
                sp.wait_ge(wo_ready, BATCHES * layer)
                load_wo(layer)
                sp.wait_ge(w2_ready, BATCHES * layer)
                sp.wait_ge(stream_ready, BATCHES * layer)
                load_ff(layer)
                if wqkv_too:
                    sp.wait_ge(proj_ready, PER_TURN * BATCHES * layer)
                    sp.wait_ge(v_ready, PER_TURN * BATCHES * layer)
                    sp.wait_ge(wqkv_in, 16 * (layer + 1))
                    load_wqkv((layer + 1) % 2, (layer + 1) * DIM)

            with sp.Fori(1, DEPTH - 1) as layer:
                next_layer(layer, True)
            next_layer(DEPTH - 1, False)
            for b in range(BATCHES):
                sp.wait_ge(tail_dve, b + 1)
                sp.dma_start(out[b].rearrange("(t p) c -> p t c", p=P),
                             x_tok[:, b * BLOCKS:(b + 1) * BLOCKS, :]).then_inc(out_stored, 16)
            sp.wait_ge(out_stored, 16 * BATCHES)


        H_DVE, H_ACT, H_PE = 29, 3, 5

        @block.gpsimd
        def _(pool):
            pool.memset(minus_half[:, :], -0.5)
            pool.memset(mean_w[:, :], 1.0 / DIM)
            pool.memset(ln_eps[:, :], LN_EPS)
            pool.memset(k_T[:, :, 0:WINDOW], 0.0)
            pool.memset(shifted[:, 0:WINDOW + 1], 0.0)
            pool.memset(ff_in[:, 0:1], 0.0).then_inc(setup_pool, 1)
            pool.wait_ge(scales_in, 16 * 6)
            pool.wait_ge(const_in, 16)

            def tables(turn):
                for n, at in enumerate((C_COS_Q, C_SIN_Q, C_COS_K, C_SIN_K)):
                    base = const[:, at:at + BLOCKS * DHEAD].rearrange("p (o u d) -> p o u d", o=1, d=DHEAD)
                    if isinstance(turn, int):
                        dst = rot[:, turn % 2:turn % 2 + 1, n, :, :]
                        scales = head_scales[:, n, turn // BATCHES:turn // BATCHES + 1, :]
                    else:
                        dst = rot[:, bass.ds(turn % 2, 1), n, :, :]
                        scales = head_scales[:, n, bass.ds(turn // BATCHES, 1), :]
                    scales = scales.rearrange("p o (u d) -> p o u d", u=1).to_broadcast([P, 1, BLOCKS, DHEAD])
                    last = pool.tensor_tensor(dst, base, scales, ALU.mult)
                last.then_inc(tables_ready, 1)

            tables(0)
            pool.wait_ge(head_dve, H_DVE * BATCHES)
            pool.wait_ge(head_pe, H_PE * BATCHES)
            pool.memset(q_diag[:, :, :, :, :], 0.0).then_inc(setup_pool, 1)

            def slot(it, nominal, u, s):
                K = PER_TURN * it + SLOTS * u + s
                if in_body(nominal, u, s, 1):
                    c = K - 1
                    cs, cu, ct = (s - 1) % SLOTS, (u if s else (u - 1) % BLOCKS), (it if s or u else it - 1)
                    pool.wait_ge(scales_in, 16 * 6)
                    pool.wait_ge(normed_ready, c + 1)
                    after(pool, rotated_ready, c - 1)
                    pool.wait_ge(tables_ready, ct + 1)
                    src = normed[:, cs % 2, :].rearrange("p (h x d) -> p h x d", x=2, d=HALF)
                    dst = sin_part[:, cs % 2, :].rearrange("p (h x d) -> p h x d", x=2, d=HALF)
                    n = 1 if cs < 2 else 3
                    table = rot[:, ct % 2:ct % 2 + 1, n, cu, :] if isinstance(ct, int) else \
                        rot[:, bass.ds(ct % 2, 1), n, cu, :]
                    for h in range(2):
                        part = table[:, :, h * HALF:(h + 1) * HALF].to_broadcast([P, 8, HALF])
                        last = pool.tensor_tensor(dst[:, :, h, :], src[:, :, 1 - h, :], part, ALU.mult)
                    last.then_inc(sin_ready, 1)
                    pool.wait_ge(sin_ready, c + 1)
                    pool.wait_ge(cos_ready, c + 1)
                    r = 4 * (cu % 2) + cs
                    pool.tensor_tensor(rotated[:, r, :], rotated[:, r, :], sin_part[:, cs % 2, :],
                                       ALU.add).then_inc(rotated_ready, 1)
                if in_body(nominal, u, s, 0):
                    pool.wait_ge(floored_ready, K + 1)
                    pool.tensor_tensor(inv_norm[:, s, :], norm2_floored[:, s, :], minus_half[:, :],
                                       ALU.pow).then_inc(inv_norm_ready, 1)
                if s == 3 and u == 1 and nominal + 1 < TURNS:
                    pool.wait_ge(scales_in, 16 * 6)
                    pool.wait_ge(cos_ready, PER_TURN * it)
                    tables(it + 1)

            turns(pool, slot)

        @block.scalar
        def _(act):
            act.wait_ge(small_in, 16 * 4)
            act.activation(tanh_gates[:, :], gates[:, :], ACT.Tanh).then_inc(setup_dve, 1)
            act.wait_ge(setup_pool, 1)
            with act.Fori(0, BATCHES) as b:
                a, d = H_ACT * b, H_DVE * b
                act.wait_ge(head_dve, d + 7)
                act.activation(h_stat[:, 4, :], h_stat[:, 3, :], ACT.Sqrt, bias=ln_eps[:, :]).then_inc(head_act, 1)
                act.wait_ge(head_dve, d + 13)
                act.activation(h_exp, h_logit, ACT.Exp).then_inc(head_act, 1)
                act.wait_ge(head_dve, d + 26)
                act.activation(h_stat[:, 4, :], h_stat[:, 3, :], ACT.Sqrt, bias=ln_eps[:, :]).then_inc(head_act, 1)

            def slot(it, nominal, u, s):
                K = PER_TURN * it + SLOTS * u + s
                if in_body(nominal, u, s, 11):
                    G = K - 11
                    act.wait_ge(o_ready, G + 1)
                    if (s, u) == (3, 2):
                        after(act, wo_ready, it)
                    keep_o(act, act.copy, 0, u, s).then_inc(o_top_kept, 1)
                if in_body(nominal, u, s, 5):
                    c = K - 5
                    cs, cu = (s - 5) % SLOTS, (SLOTS * u + s - 5) // SLOTS % BLOCKS
                    act.wait_ge(qkT_ready, c + 1)
                    after(act, s_ready, c - cs - 4)
                    if cs == 0 and nominal <= 1:
                        act.wait_ge(setup_pool, 2)
                    if cs < 2:
                        keep_q(act.copy, 0, cs, cu).then_inc(q_top_ready, 1)
                    else:
                        j = cs - 2
                        act.copy(k_T[:, 4 * j:4 * j + 4, WINDOW + P * cu:WINDOW + P * (cu + 1)],
                                 ps[:, PS_QKT, :].rearrange("p (j t) -> p j t", j=4)).then_inc(k_ready, 1)
                if in_body(nominal, u, s, 1):
                    c = K - 1
                    cs, cu = (s - 1) % SLOTS, (SLOTS * u + s - 1) // SLOTS % BLOCKS
                    act.wait_ge(v_ready, c + 1)
                    after(act, o_ready, c - 15)
                    act.copy(v_tile[:, 2 * cu + cs // 2, 512 * (cs % 2):512 * (cs % 2) + 512],
                             ps[0:KT, PS_V, :]).then_inc(v_kept, 1)
                if in_body(nominal, u, s, 8):
                    G = K - 8
                    act.wait_ge(neg_max_ready, G + 1)
                    after(act, pT_ready, G - 1)
                    for j in range(4):
                        last = act.activation(probs[:, s % 2, j, :], ps[:, PS_S, j * KT:(j + 1) * KT], ACT.Exp,
                                              bias=neg_max[:, s % 2, j:j + 1], scale=QK_SCALE,
                                              accum_out=row_sum[:, s % 2, j:j + 1])
                    last.then_inc(exp_ready, 1)
                if in_body(nominal, u, s, 0):
                    act.wait_ge(proj_ready, K + 1)
                    after(act, norm2_ready, K - 1)
                    act.activation(squares[:, s % 2, :], ps[:, s % 2, :], ACT.Square).then_inc(squares_ready, 1)
                if in_body(nominal, u, s, 9):
                    G = K - 9
                    act.wait_ge(pT_ready, G + 1)
                    after(act, o_ready, G - 1)
                    act.copy(probs_T[:, (s - 1) % 2, :, :],
                             ps[0:KT, PS_PT, :].rearrange("p (j q) -> p j q", j=4)).then_inc(pT_kept, 1)
                t = ff_turn(it, nominal, 1)
                if t is not None and (u, s) == (3, 1):
                    act.wait_ge(centred, t + 1)
                    act.activation(ff_std[:, :], ff_in[:, :], ACT.Square).then_inc(ff_sq_ready, 1)
                if t is not None and (u, s) == (3, 2):
                    act.wait_ge(var_ready, t + 1)
                    after(act, ff_norm_ready, t)
                    act.activation(ff_std[:, :], ps[:, PS_FF, :], ACT.Sqrt, bias=ln_eps[:, :]).then_inc(std_ready, 1)
                t = ff_turn(it, nominal, 2)
                if t is not None and (u, s) == (0, 3):
                    act.wait_ge(gate_kept, 3 * t + 3)
                    act.activation(gate_sb[:, :, :], gate_sb[:, :, :], ACT.Gelu).then_inc(gelu_ready, 1)

            turns(act, slot)

        @block.vector
        def _(dve):
            dve.wait_ge(const_in, 16)
            dve.tensor_copy(ident_bf[:, :], ident)
            dve.tensor_copy(band_bf[:, :, :], const[:, C_BAND:C_BAND + 2 * KT].rearrange("p (a k) -> p a k", a=2))
            dve.memset(gate_sb[:, :, :], 0.0)
            dve.wait_ge(small_in, 16 * 4)
            bias = logit_bias[:, :, :].rearrange("p b k -> p (b k)")
            dve.tensor_copy(bias, mask_i[:, :]).then_inc(setup_dve, 1)
            dve.wait_ge(setup_dve, 2)
            dve.tensor_scalar(bias, bias, -1.0, 1e30, ALU.add, ALU.mult).then_inc(setup_dve, 1)
            dve.wait_ge(head_pe, 1)
            head_of_row = const[:, C_HEADK:C_HEADK + XHEADS].rearrange("p (h k) -> p h k", k=1)
            for b in range(BATCHES):
                dve.tensor_tensor(key_diag[:, b, :].rearrange("p (h k) -> p h k", h=XHEADS),
                                  ps[:, 0, b * XKEYS:(b + 1) * XKEYS].rearrange("p (h k) -> p h k", h=1)
                                  .to_broadcast([P, XHEADS, XKEYS]),
                                  head_of_row.to_broadcast([P, XHEADS, XKEYS]), ALU.mult)
            dve.wait_ge(ctx_in, 16 * 5)
            for b in range(BATCHES):
                dve.tensor_tensor(value_diag[:, 2 * b:2 * b + 2, :],
                                  ctx_v[:, b:b + 1, :].to_broadcast([P, 2, DIM]),
                                  const[:, C_HEADV:C_HEADV + 2 * P].rearrange("p (a c) -> p a c", a=2), ALU.mult)
            dve.wait_ge(setup_dve, 3)
            last = dve.tensor_scalar(bias, bias, xbias[:, 0:1], None, ALU.add)
            last.then_inc(setup_dve, 1)
            dve.wait_ge(setup_dve, 4)
            dve.wait_ge(x_in, 16)

            with dve.Fori(0, BATCHES) as b:
                base, n = H_DVE * b, [0]
                tiles = x_tok[:, bass.ds(b * BLOCKS, BLOCKS), :]

                def step(ins):
                    n[0] += 1
                    ins.then_inc(head_dve, 1)
                    dve.wait_ge(head_dve, base + n[0])

                def stat(i):
                    return h_stat[:, i, :]

                def wide(ap, shape):
                    return ap.rearrange("p (a c) -> p a c", c=1).to_broadcast(shape)

                def layernorm(act_count):
                    step(dve.tensor_reduce(stat(0), h_x, AX, ALU.add))
                    step(dve.tensor_scalar(stat(1), stat(0), 1.0 / DIM, None, ALU.mult))
                    step(dve.tensor_tensor(h_x, h_x, wide(stat(1), [P, BLOCKS, DIM]), ALU.subtract))
                    step(dve.tensor_tensor(h_sq, h_x, h_x, ALU.mult))
                    step(dve.tensor_reduce(stat(2), h_sq, AX, ALU.add))
                    step(dve.tensor_scalar(stat(3), stat(2), 1.0 / DIM, None, ALU.mult))
                    dve.wait_ge(head_act, H_ACT * b + act_count)
                    step(dve.reciprocal(stat(5), stat(4)))
                    step(dve.tensor_tensor(h_x, h_x, wide(stat(5), [P, BLOCKS, DIM]), ALU.mult))

                step(dve.tensor_scalar(h_x, tiles, 1.0, None, ALU.mult))
                layernorm(1)
                dve.wait_ge(head_pe, H_PE * b + 2)
                step(dve.tensor_copy(h_T, ps[:, 1, :].rearrange("p (a c) -> p a c", c=P)))
                dve.wait_ge(head_pe, H_PE * b + 3)
                logits = ps[:, 2:4, :].rearrange("p a n -> p (a n)").rearrange("p (m k) -> p m k", k=XKEYS)
                lg = h_logit.rearrange("p (m k) -> p m k", k=XKEYS)
                ex = h_exp.rearrange("p (m k) -> p m k", k=XKEYS)
                rows32 = [P, BLOCKS * XHEADS, XKEYS]
                step(dve.scalar_tensor_tensor(lg, logits, XSCALE, logit_bias[:, bass.ds(b, 1), :].to_broadcast(rows32),
                                              ALU.mult, ALU.add))
                step(dve.tensor_reduce(h_red, lg, AX, ALU.max))
                step(dve.tensor_tensor(lg, lg, wide(h_red, rows32), ALU.subtract))
                dve.wait_ge(head_act, H_ACT * b + 2)
                step(dve.tensor_reduce(h_red, ex, AX, ALU.add))
                step(dve.reciprocal(h_inv, h_red))
                step(dve.tensor_tensor(ex, ex, wide(h_inv, rows32), ALU.mult))
                dve.wait_ge(head_pe, H_PE * b + 4)
                step(dve.tensor_copy(h_expT, ps[:, 4:6, :].rearrange("p a n -> p (a n)")))
                dve.wait_ge(head_pe, H_PE * b + 5)
                step(dve.tensor_scalar(h_x, ps[:, 6, :].rearrange("p (a c) -> p a c", c=P), tanh_gates[:, 0:1], None,
                                       ALU.mult))
                step(dve.tensor_tensor(h_x, h_x, tiles, ALU.add))
                step(dve.tensor_scalar(tiles, h_x, 1.0, None, ALU.mult))
                layernorm(3)
                dve.wait_ge(head_pe, H_PE * b + 6)
                step(dve.tensor_copy(pick(stream, b), ps[:, 7, :]))

            def shift(it, u):
                src = pick(stream, it % BATCHES)
                lo, at = P * u, WINDOW + P * u
                dve.tensor_copy(shifted[0:QT, at:at + P], src[0:QT, lo:lo + P])
                first = 1 if u == 0 else 0
                dve.tensor_copy(shifted[QT:P, at + first:at + P], src[QT:P, lo - 1 + first:lo + P - 1]
                                ).then_inc(shifted_ready, 1)

            shift(0, 0)
            shift(0, 1)

            def slot(it, nominal, u, s):
                K = PER_TURN * it + SLOTS * u + s
                if in_body(nominal, u, s, 11):
                    G = K - 11
                    dve.wait_ge(o_ready, G + 1)
                    if (s, u) == (3, 2):
                        after(dve, wo_ready, it)
                    keep_o(dve, dve.tensor_copy, 1, u, s).then_inc(o_low_kept, 1)
                if in_body(nominal, u, s, 5) and (s - 5) % SLOTS < 2:
                    c = K - 5
                    cs, cu = (s - 5) % SLOTS, (SLOTS * u + s - 5) // SLOTS % BLOCKS
                    dve.wait_ge(qkT_ready, c + 1)
                    after(dve, s_ready, c - cs - 4)
                    if cs == 0 and nominal <= 1:
                        dve.wait_ge(setup_pool, 2)
                    keep_q(dve.tensor_copy, 1, cs, cu).then_inc(q_low_ready, 1)
                if s == 0 and nominal * BLOCKS + u + 2 < TURNS * BLOCKS:
                    after(dve, proj_ready, K)
                    after(dve, v_ready, K)
                    shift(it if u < 2 else it + 1, (u + 2) % BLOCKS)
                if in_body(nominal, u, s, 8):
                    G = K - 8
                    dve.wait_ge(s_ready, G + 1)
                    scores = ps[:, PS_S, 0:4 * KT].rearrange("p (j k) -> p j k", j=4)
                    dve.tensor_reduce(row_max[:, s % 2, :], scores, AX, ALU.max).then_inc(max_ready, 1)
                    dve.wait_ge(max_ready, G + 1)
                    dve.tensor_scalar(neg_max[:, s % 2, :], row_max[:, s % 2, :], -QK_SCALE, None,
                                      ALU.mult).then_inc(neg_max_ready, 1)
                feed_forward(it, nominal, u, s)
                if in_body(nominal, u, s, 1):
                    c = K - 1
                    cs, cu, ct = (s - 1) % SLOTS, (u if s else (u - 1) % BLOCKS), (it if s or u else it - 1)
                    dve.wait_ge(inv_norm_ready, c + 1)
                    after(dve, sin_ready, c - 1)
                    heads = normed[:, cs % 2, :].rearrange("p (h d) -> p h d", h=8)
                    dve.tensor_tensor(heads, ps[:, cs % 2, :].rearrange("p (h d) -> p h d", h=8),
                                      inv_norm[:, cs, :].rearrange("p (h d) -> p h d", d=1)
                                      .to_broadcast([P, 8, DHEAD]), ALU.mult).then_inc(normed_ready, 1)
                    dve.wait_ge(normed_ready, c + 1)
                    dve.wait_ge(tables_ready, ct + 1)
                    after(dve, qkT_ready, c - 7)
                    n = 0 if cs < 2 else 2
                    table = rot[:, ct % 2:ct % 2 + 1, n, cu, :] if isinstance(ct, int) else \
                        rot[:, bass.ds(ct % 2, 1), n, cu, :]
                    dve.tensor_tensor(rotated[:, 4 * (cu % 2) + cs, :].rearrange("p (h d) -> p h d", h=8), heads,
                                      table.to_broadcast([P, 8, DHEAD]), ALU.mult).then_inc(cos_ready, 1)
                if in_body(nominal, u, s, 8):
                    G, r = K - 8, s % 2
                    dve.wait_ge(exp_ready, G + 1)
                    dve.reciprocal(inv_sum[:, r, :], row_sum[:, r, :]).then_inc(inv_sum_ready, 1)
                    dve.wait_ge(inv_sum_ready, G + 1)
                    dve.tensor_tensor(probs[:, r, :, :], probs[:, r, :, :],
                                      inv_sum[:, r, :].rearrange("p (j k) -> p j k", k=1).to_broadcast([P, 4, KT]),
                                      ALU.mult).then_inc(probs_ready, 1)
                if in_body(nominal, u, s, 0):
                    dve.wait_ge(squares_ready, K + 1)
                    dve.tensor_reduce(norm2[:, s, :], squares[:, s % 2, :].rearrange("p (h d) -> p h d", h=8), AX,
                                      ALU.add).then_inc(norm2_ready, 1)
                    dve.wait_ge(norm2_ready, K + 1)
                    dve.tensor_scalar(norm2_floored[:, s, :], norm2[:, s, :], NORM_FLOOR ** 2, None,
                                      ALU.max).then_inc(floored_ready, 1)

            def feed_forward(it, nominal, u, s):
                t = ff_turn(it, nominal, 1)
                if t is not None and (u, s) == (2, 3):
                    dve.wait_ge(wo_ready, t + 1)
                    dve.tensor_tensor(mid[:, :], ps[:, PS_FF, :], pick(stream, t % BATCHES), ALU.add
                                      ).then_inc(mid_ready, 1)
                    dve.wait_ge(mid_ready, t + 1)
                    dve.tensor_copy(ff_in[0:QT, :], mid[0:QT, :])
                    dve.memset(ff_in[QT:P, 0:1], 0.0)
                    dve.tensor_copy(ff_in[QT:P, 1:TOKENS], mid[QT:P, 0:TOKENS - 1]).then_inc(ff_in_ready, 1)
                if t is not None and (u, s) == (3, 0):
                    dve.wait_ge(mean_ready, t + 1)
                    dve.tensor_tensor(ff_in[:, :], ff_in[:, :], ps[:, PS_FF, :], ALU.subtract).then_inc(centred, 1)
                if t is not None and (u, s) == (3, 3):
                    dve.wait_ge(std_ready, t + 1)
                    dve.reciprocal(ff_std[:, :], ff_std[:, :]).then_inc(ff_dve, 1)
                    dve.wait_ge(ff_dve, 2 * t + 1)
                    dve.wait_ge(ff_w_in, FF_LOADS * (t // BATCHES + 1))
                    dve.scalar_tensor_tensor(ff_norm[:, :], ff_in[:, :], ln_g_sb[:, 0:1], ff_std[:, :],
                                             ALU.mult, ALU.mult).then_inc(ff_dve, 1)
                    dve.wait_ge(ff_dve, 2 * t + 2)
                    dve.tensor_scalar(ff_norm[:, :], ff_norm[:, :], ln_b_sb[:, 0:1], None, ALU.add
                                      ).then_inc(ff_norm_ready, 1)
                t = ff_turn(it, nominal, 2)
                if t is None:
                    return
                if (u, s) in ((0, 0), (0, 1), (0, 2)):
                    j = s
                    m = HID_PARTS[j]
                    dve.wait_ge(gate_ready, 3 * t + j + 1)
                    after(dve, w2_ready, t)
                    dve.tensor_scalar(gate_sb[0:m, j, :], ps[0:m, PS_FF, :], b1_sb[0:m, 1, j:j + 1], None, ALU.add
                                      ).then_inc(gate_kept, 1)
                if (u, s) in ((1, 0), (1, 1), (1, 2)):
                    m = HID_PARTS[s]
                    dve.wait_ge(lin_ready, 3 * t + s + 1)
                    dve.wait_ge(gelu_ready, t + 1)
                    dve.scalar_tensor_tensor(gate_sb[0:m, s, :], ps[0:m, PS_FF, :], b1_sb[0:m, 0, s:s + 1],
                                             gate_sb[0:m, s, :], ALU.add, ALU.mult).then_inc(hidden_ready, 1)
                if (u, s) == (1, 3):
                    dve.wait_ge(w2_ready, t + 1)
                    dve.scalar_tensor_tensor(pick(stream, t % BATCHES), ps[:, PS_FF, :], b2_sb[:, 0:1], mid[:, :],
                                             ALU.add, ALU.add).then_inc(stream_ready, 1)

            turns(dve, slot)

            for b in range(BATCHES):
                tiles = x_tok[:, b * BLOCKS:(b + 1) * BLOCKS, :]
                dve.wait_ge(tail_pe, b + 1)
                dve.scalar_tensor_tensor(tiles, ps[:, b, :].rearrange("p (t c) -> p t c", c=DIM),
                                         tanh_gates[:, 1:2], tiles, ALU.mult, ALU.add).then_inc(tail_dve, 1)

        @block.tensor
        def _(pe):
            pe.wait_ge(const_in, 16)
            pe.wait_ge(ctx_in, 16 * 5)
            for b in range(BATCHES):
                last = nc.tensor.transpose(ps[:, 0, b * XKEYS:(b + 1) * XKEYS], ctx_k[:, b, :], ident[0:XKEYS, 0:XKEYS])
            last.then_inc(head_pe, 1)
            pe.wait_ge(setup_dve, 4)
            with pe.Fori(0, BATCHES) as b:
                def transposed(bank, src):
                    for i in range(BLOCKS):
                        last = nc.tensor.transpose(ps[:, bank, i * P:(i + 1) * P], src[:, i, :], ident)
                    return last

                d = H_DVE * b
                pe.wait_ge(head_dve, d + 9)
                transposed(1, h_x).then_inc(head_pe, 1)
                pe.wait_ge(head_dve, d + 10)
                for i in range(BLOCKS):
                    last = nc.tensor.matmul(ps[:, 2 + i // 2, 256 * (i % 2):256 * (i % 2) + 256], h_T[:, i, :],
                                            pick(key_diag, b), start=True, stop=True)
                last.then_inc(head_pe, 1)
                pe.wait_ge(head_dve, d + 16)
                for i in range(2 * BLOCKS):
                    last = nc.tensor.transpose(ps[:, 4 + i // 4, P * (i % 4):P * (i % 4) + P],
                                               h_exp[:, P * i:P * (i + 1)], ident)
                last.then_inc(head_pe, 1)
                pe.wait_ge(head_dve, d + 17)
                for i in range(BLOCKS):
                    for j in range(2):
                        last = nc.tensor.matmul(ps[:, 6, P * i:P * (i + 1)], h_expT[:, P * (2 * i + j):P * (2 * i + j + 1)],
                                                pick(value_diag, 2 * b + j), start=(j == 0), stop=(j == 1))
                last.then_inc(head_pe, 1)
                pe.wait_ge(head_dve, d + 28)
                transposed(7, h_x).then_inc(head_pe, 1)

            pe.wait_ge(head_dve, H_DVE * BATCHES)
            pe.wait_ge(setup_pool, 1)

            def slot(it, nominal, u, s):
                K = PER_TURN * it + SLOTS * u + s
                half = s % 2
                feed_forward(it, nominal, u, s)
                if in_body(nominal, u, s, 8):
                    G = K - 8
                    gu = (u - 2) % BLOCKS
                    pe.wait_ge(q_top_ready, 2 * (BLOCKS * it + u - 2) + half + 1)
                    pe.wait_ge(q_low_ready, 2 * (BLOCKS * it + u - 2) + half + 1)
                    pe.wait_ge(k_ready, 2 * (BLOCKS * it + u - 2) + half + 1)
                    after(pe, exp_ready, G)
                    first = 0 if gu == 0 and s < 2 else 1
                    nc.tensor.matmul(ps[:, PS_S, 0:4 * KT].rearrange("p (j k) -> p j k", j=4), ident_bf[:, :],
                                     band_bf[:, first:first + 1, :].to_broadcast([P, 4, KT]), start=True, stop=False,
                                     skip_group_check=True)
                    t0 = P * gu + QT * (s // 2)
                    for j in range(4):
                        pair = 4 * half + j
                        last = nc.tensor.matmul(ps[:, PS_S, j * KT:(j + 1) * KT], q_diag[:, gu % 2, s // 2, pair, :],
                                                k_T[:, pair, t0:t0 + KT], start=False, stop=(j == 3),
                                                skip_group_check=True)
                    last.then_inc(s_ready, 1)
                if in_body(nominal, u, s, 0):
                    pe.wait_ge(wqkv_in, 16 * (it // BATCHES + 1))
                    pe.wait_ge(shifted_ready, BLOCKS * it + u + 1)
                    after(pe, normed_ready, K - 1)
                    nc.tensor.matmul(ps[:, s % 2, :], shifted[:, WINDOW + P * u:WINDOW + P * (u + 1)],
                                     weights(it, 512 * s), start=True, stop=True).then_inc(proj_ready, 1)
                if in_body(nominal, u, s, 9):
                    G = K - 9
                    pe.wait_ge(probs_ready, G + 1)
                    after(pe, pT_kept, G)
                    for j in range(4):
                        last = nc.tensor.transpose(ps[0:KT, PS_PT, P * j:P * (j + 1)], probs[:, (s - 1) % 2, j, :], ident)
                    last.then_inc(pT_ready, 1)
                if in_body(nominal, u, s, 0):
                    after(pe, v_kept, K)
                    t0 = P * u + QT * (s // 2)
                    nc.tensor.matmul(ps[0:KT, PS_V, :], shifted[:, t0:t0 + KT], weights(it, 2 * INNER + 512 * half),
                                     start=True, stop=True).then_inc(v_ready, 1)
                if in_body(nominal, u, s, 4):
                    c = K - 4
                    pe.wait_ge(rotated_ready, c + 1)
                    blocks_before = BLOCKS * it + u - 1
                    if s < 3:
                        after(pe, q_top_ready, 2 * blocks_before + min(s, 2))
                        after(pe, q_low_ready, 2 * blocks_before + min(s, 2))
                    after(pe, k_ready, 2 * blocks_before + max(s - 2, 0))
                    for j in range(4):
                        last = nc.tensor.transpose(ps[:, PS_QKT, P * j:P * (j + 1)],
                                                   rotated[:, 4 * ((u - 1) % 2) + s, P * j:P * (j + 1)], ident)
                    last.then_inc(qkT_ready, 1)
                if in_body(nominal, u, s, 10):
                    G = K - 10
                    g = (SLOTS * u + s - 10) % PER_TURN
                    pe.wait_ge(pT_kept, G + 1)
                    after(pe, o_top_kept, G)
                    after(pe, o_low_kept, G)
                    pe.wait_ge(v_kept, G + 1)
                    for j in range(4):
                        pair = 4 * (g % 2) + j
                        last = nc.tensor.matmul(ps[:, PS_O, P * j:P * (j + 1)], v_tile[:, g // 2, P * pair:P * (pair + 1)],
                                                probs_T[:, s % 2, j, :], start=True, stop=True)
                    last.then_inc(o_ready, 1)

            def weights(it, at):
                if isinstance(it, int):
                    return wqkv_sb[:, it // BATCHES % 2, at:at + 512]
                return wqkv_sb[:, bass.ds(it // BATCHES % 2, 1), at:at + 512].rearrange("p a n -> p (a n)")

            def feed_forward(it, nominal, u, s):
                bank = ps[:, PS_FF, :]
                t = ff_turn(it, nominal, 1)
                if t is not None and (u, s) in ((2, 2), (2, 3)):
                    part = s - 2
                    if part == 0:
                        pe.wait_ge(wo_in, 16 * (t // BATCHES + 1))
                        after(pe, stream_ready, t)
                    pe.wait_ge(o_top_kept, PER_TURN * t + 15 + part)
                    pe.wait_ge(o_low_kept, PER_TURN * t + 15 + part)
                    for j in range(4 * part, 4 * part + 4):
                        last = nc.tensor.matmul(bank, wo_sb[:, j, :], attn_T[:, j, :], start=(j == 0),
                                                stop=(j == PAIRS - 1))
                    if part == 1:
                        last.then_inc(wo_ready, 1)
                if t is not None and (u, s) == (3, 0):
                    pe.wait_ge(ff_in_ready, t + 1)
                    nc.tensor.matmul(bank, mean_w[:, :], ff_in[:, :], start=True, stop=True).then_inc(mean_ready, 1)
                if t is not None and (u, s) == (3, 2):
                    pe.wait_ge(ff_sq_ready, t + 1)
                    nc.tensor.matmul(bank, mean_w[:, :], ff_std[:, :], start=True, stop=True).then_inc(var_ready, 1)
                t = ff_turn(it, nominal, 2)
                if t is None:
                    return
                at = (0, HID_PARTS[0], HID_PARTS[0] + HID_PARTS[1])
                if (u, s) in ((0, 0), (0, 1), (0, 2)):
                    pe.wait_ge(ff_norm_ready, t + 1)
                    pe.wait_ge(ff_w_in, FF_LOADS * (t // BATCHES + 1))
                    after(pe, gate_kept, 3 * t + s)
                    nc.tensor.matmul(bank[0:HID_PARTS[s]], w1_sb[:, HIDDEN + at[s]:HIDDEN + at[s] + HID_PARTS[s]],
                                     ff_norm[:, :], start=True, stop=True).then_inc(gate_ready, 1)
                if (u, s) in ((1, 0), (1, 1), (1, 2)):
                    pe.wait_ge(gate_kept, 3 * t + 3)
                    after(pe, hidden_ready, 3 * t + s)
                    nc.tensor.matmul(bank[0:HID_PARTS[s]], w1_sb[:, at[s]:at[s] + HID_PARTS[s]],
                                     ff_norm[:, :], start=True, stop=True).then_inc(lin_ready, 1)
                if (u, s) == (1, 3):
                    pe.wait_ge(hidden_ready, 3 * t + 3)
                    for j, m in enumerate(HID_PARTS):
                        last = nc.tensor.matmul(bank, w2_sb[0:m, j, :], gate_sb[0:m, j, :], start=(j == 0), stop=(j == 2))
                    last.then_inc(w2_ready, 1)

            turns(pe, slot)

            pe.wait_ge(stream_ready, TURNS)
            for b in range(BATCHES):
                for i in range(BLOCKS):
                    last = nc.tensor.transpose(ps[:, b, i * P:(i + 1) * P], stream[:, b, i * P:(i + 1) * P], ident)
                last.then_inc(tail_pe, 1)


_INS = ['x', 'ctx_2048', 'mask_BxS2_ik0', 'g_xattn', 'g_ffn', 'L0_xattn_b', 'L0_ffn_Wqkv', 'L0_ffn_q_scale',
        'L0_ffn_k_scale', 'L0_ffn_Wo', 'L0_ffn_ln_g', 'L0_ffn_ln_b', 'L0_ffn_W1', 'L0_ffn_b1', 'L0_ffn_W2',
        'L0_ffn_b2']
_SHAPES = {'L0_ffn_Wqkv': (DEPTH * DIM, 3 * INNER), 'L0_ffn_Wo': (DEPTH * INNER, DIM),
           'L0_ffn_W1': (DEPTH * DIM, 2 * HIDDEN), 'L0_ffn_W2': (DEPTH * HIDDEN, DIM),
           'L0_ffn_ln_g': (DEPTH * DIM, 1), 'L0_ffn_ln_b': (DEPTH * DIM, 1), 'L0_ffn_b2': (DEPTH * DIM, 1),
           'L0_ffn_b1': (DEPTH * 2 * HIDDEN, 1)}


def kernel(**inputs):
    import numpy as _np
    import concourse.bacc as _bacc
    from concourse import mybir as _mybir
    from concourse.bass_utils import run_bass_kernel_spmd as _run

    nc = _bacc.Bacc("TRN2", target_bir_lowering=False, num_devices=1)
    arrays, args = {}, []
    for name in _INS:
        a = _np.ascontiguousarray(inputs[name])
        a = a.reshape(_SHAPES.get(name, a.shape))
        arrays[f"in_{name}_dram"] = a
        args.append(nc.dram_tensor(f"in_{name}_dram", a.shape, _mybir.dt.from_np(a.dtype), kind="ExternalInput").ap())
    arrays["consts_dram"] = shape_constants()
    args.append(nc.dram_tensor("consts_dram", (P, C_END), F32, kind="ExternalInput").ap())
    args.append(nc.dram_tensor("out_dram", (BATCHES, TOKENS, DIM), F32, kind="ExternalOutput").ap())
    build(nc, *args)
    r = _run(nc, [arrays], core_ids=[0])
    return r.results[0]["out_dram"]
```

```python
from contextlib import ExitStack

import numpy as np

import concourse.bass as bass
from concourse import mybir

F32 = mybir.dt.float32
BF16 = mybir.dt.bfloat16
F32R = mybir.dt.float32r
I32 = mybir.dt.int32
ALU = mybir.AluOpType
ACT = mybir.ActivationFunctionType
AX = mybir.AxisListType.X

P = 128
BATCHES, TOKENS, DIM = 4, 512, 128
DEPTH, HEADS, DHEAD, WINDOW = 6, 16, 64, 32
HALF = DHEAD // 2
INNER = HEADS * DHEAD
HIDDEN = int(DIM * 4 * 2 / 3)
QK_SCALE = 8.0
NORM_FLOOR = 1e-12
LN_EPS = 1e-5
BLOCKS = TOKENS // P
SLOTS = 4
PAIRS = HEADS // 2
QT = 64
KT = QT + WINDOW
TURNS = DEPTH * BATCHES
PER_TURN = BLOCKS * SLOTS
HID_PARTS = (114, 114, 113)
HID_MAX = 114
MASKED = -float(2 ** 100)
PIECES = 8
PIECE = 3 * INNER // PIECES
V_LAG = 8
XHEADS, XKEYS = 8, 32
XDEPTH = DIM // XHEADS
XSCALE = float(XDEPTH) ** -0.5

C_IDENT = 0
C_BAND = C_IDENT + P
C_HEADK = C_BAND + 2 * KT
C_HEADV = C_HEADK + XHEADS
C_COS_Q = C_HEADV + 2 * P
C_SIN_Q = C_COS_Q + BLOCKS * DHEAD
C_COS_K = C_SIN_Q + BLOCKS * DHEAD
C_SIN_K = C_COS_K + BLOCKS * DHEAD
C_END = C_SIN_K + BLOCKS * DHEAD


def shape_constants():
    c = np.zeros((P, C_END), np.float32)
    row = np.arange(P)[:, None]
    c[:, C_IDENT:C_IDENT + P] = np.eye(P)
    key = np.arange(KT)[None, :]
    query = row % QT
    seen = (key >= query) & (key <= query + WINDOW)
    c[:, C_BAND:C_BAND + KT] = np.where(seen & (key >= WINDOW), 0.0, MASKED)
    c[:, C_BAND + KT:C_BAND + 2 * KT] = np.where(seen, 0.0, MASKED)
    c[:, C_HEADK:C_HEADK + XHEADS] = row // XDEPTH == np.arange(XHEADS)[None, :]
    for j in range(2):
        c[:, C_HEADV + j * P:C_HEADV + (j + 1) * P] = row // XKEYS + 4 * j == np.arange(P)[None, :] // XDEPTH
    half = np.arange(0, DHEAD, 2, dtype=np.float32)
    inv_freq = (1.0 / 10000.0 ** (half.astype(np.float64) / DHEAD)).astype(np.float32)
    t = np.arange(TOKENS, dtype=np.float32)
    freqs = (t[:, None] * inv_freq[None, :]).astype(np.float32).astype(np.float64)
    base = (half.astype(np.float64) + 0.4 * DHEAD) / (1.4 * DHEAD)
    power = (t.astype(np.float64) - TOKENS // 2) / (WINDOW // 2)
    scale = base[None, :] ** power[:, None]
    sign = np.concatenate([-np.ones(HALF), np.ones(HALF)])
    for at_cos, at_sin, s in ((C_COS_Q, C_SIN_Q, QK_SCALE * scale), (C_COS_K, C_SIN_K, 1.0 / scale)):
        cos = np.tile(np.cos(freqs) * s, 2)
        sin = np.tile(np.sin(freqs) * s, 2) * sign
        for at, table in ((at_cos, cos), (at_sin, sin)):
            c[:, at:at + BLOCKS * DHEAD] = table.reshape(BLOCKS, P, DHEAD).transpose(1, 0, 2).reshape(P, -1)
    return c


def build(nc, x, ctx_mem, mask, g_xattn, g_ffn, xb, wqkv, q_scale, k_scale, wo, ln_g, ln_b, w1, b1, w2, b2,
          consts, out):
    ctx = ExitStack()
    with ctx:
        def sb(name, shape, dt=F32):
            return ctx.enter_context(nc.sbuf_tensor(name, shape, dt))

        def sem(name):
            return ctx.enter_context(nc.semaphore(name))

        const = sb("const", [P, C_END])
        ident = const[:, C_IDENT:C_IDENT + P]
        ident_bf = sb("ident_bf", [P, P], BF16)
        band_bf = sb("band_bf", [P, 2, KT], BF16)
        mean_w = sb("mean_w", [P, P])
        ln_eps = sb("ln_eps", [P, 1])
        minus_half = sb("minus_half", [P, 8])
        gates = sb("gates", [P, 2])
        tanh_gates = sb("tanh_gates", [P, 2])
        x_tok = sb("x_tok", [P, BATCHES * BLOCKS, DIM])
        stream = sb("stream", [P, BATCHES, TOKENS])
        wqkv_high = sb("wqkv_high", [P, 2 * 3 * INNER], F32R)
        wqkv_low = sb("wqkv_low", [P, 2 * 3 * INNER], F32R)
        wqkv_raw = sb("wqkv_raw", [P, 2, PIECE])
        wo_sb = sb("wo_sb", [P, PAIRS, DIM])
        w1_sb = sb("w1_sb", [P, 2 * HIDDEN])
        w2_sb = sb("w2_sb", [HID_MAX, 3, DIM])
        ln_g_sb = sb("ln_g_sb", [P, 1])
        ln_b_sb = sb("ln_b_sb", [P, 1])
        b2_sb = sb("b2_sb", [P, 1])
        b1_sb = sb("b1_sb", [HID_MAX, 2, 3])
        head_scales = sb("head_scales", [P, 4, DEPTH, DHEAD])
        rot = sb("rot", [P, 2, 4, BLOCKS, DHEAD])
        shifted_high = sb("shifted_high", [P, BLOCKS, WINDOW + P], F32R)
        shifted_low = sb("shifted_low", [P, BLOCKS, WINDOW + P], F32R)
        squares = sb("squares", [P, 2, 512])
        norm2 = sb("norm2", [P, 4, 8])
        norm2_floored = sb("norm2_floored", [P, 4, 8])
        inv_norm = sb("inv_norm", [P, 4, 8])
        normed = sb("normed", [P, 2, 512])
        sin_part = sb("sin_part", [P, 2, 512])
        rotated = sb("rotated", [P, 4, 512])
        q_diag = sb("q_diag", [P, 2, 2, PAIRS, P])
        k_T = sb("k_T", [P, PAIRS, WINDOW + TOKENS])
        v_tile = sb("v_tile", [KT, 2, INNER])
        neg_max = sb("neg_max", [P, 2, 4])
        row_sum = sb("row_sum", [P, 2, 4])
        inv_sum = sb("inv_sum", [P, 2, 4])
        probs = sb("probs", [P, 2, 4, KT])
        probs_T = sb("probs_T", [KT, 2, 4, P])
        attn_T = sb("attn_T", [P, PAIRS, TOKENS])
        mid = sb("mid", [P, TOKENS])
        ff_in = sb("ff_in", [P, TOKENS])
        ff_std = sb("ff_std", [P, TOKENS])
        gate_sb = sb("gate_sb", [HID_MAX, 3, TOKENS])

        ps = ctx.enter_context(nc.psum_tensor("ps", [P, 8, 512], F32))
        PS_V, PS_QKT, PS_S, PS_PT, PS_O, PS_FF = 2, 3, 4, 5, 6, 7

        const_in, x_in, ctx_in, small_in, scales_in = (sem(n) for n in ("const_in", "x_in", "ctx_in", "small_in",
                                                                        "scales_in"))
        wqkv_in = [sem("wqkv_first_in"), sem("wqkv_second_in")]
        wo_in, ff_w_in, out_stored = (sem(n) for n in ("wo_in", "ff_w_in", "out_stored"))
        setup_dve, setup_pool = sem("setup_dve"), sem("setup_pool")
        head_dve, head_act, head_pe = sem("head_dve"), sem("head_act"), sem("head_pe")
        tail_pe, tail_dve = sem("tail_pe"), sem("tail_dve")
        tables_ready, high_ready, shifted_ready = sem("tables_ready"), sem("high_ready"), sem("shifted_ready")
        wqkv_high_ready, wqkv_low_ready = sem("wqkv_high_ready"), sem("wqkv_low_ready")
        proj_ready, v_ready, qkT_ready, s_ready, pT_ready, o_ready = (
            sem(n) for n in ("proj_ready", "v_ready", "qkT_ready", "s_ready", "pT_ready", "o_ready"))
        squares_ready, norm2_ready, floored_ready, inv_norm_ready, normed_ready = (
            sem(n) for n in ("squares_ready", "norm2_ready", "floored_ready", "inv_norm_ready", "normed_ready"))
        cos_ready, sin_ready, rotated_ready = sem("cos_ready"), sem("sin_ready"), sem("rotated_ready")
        q_top_ready, q_low_ready, k_ready, v_kept = (
            sem(n) for n in ("q_top_ready", "q_low_ready", "k_ready", "v_kept"))
        neg_max_ready, exp_ready, inv_sum_ready, probs_ready, pT_kept = (
            sem(n) for n in ("neg_max_ready", "exp_ready", "inv_sum_ready", "probs_ready", "pT_kept"))
        o_top_kept, o_low_kept = sem("o_top_kept"), sem("o_low_kept")
        wo_ready, mean_ready, var_ready, gate_ready, lin_ready, w2_ready = (
            sem(n) for n in ("wo_ready", "mean_ready", "var_ready", "gate_ready", "lin_ready", "w2_ready"))
        mid_ready, ff_in_ready, centred, ff_sq_ready, std_ready, ff_dve = (
            sem(n) for n in ("mid_ready", "ff_in_ready", "centred", "ff_sq_ready", "std_ready", "ff_dve"))
        ff_norm_ready, gate_kept, gelu_ready, hidden_ready, stream_ready = (
            sem(n) for n in ("ff_norm_ready", "gate_kept", "gelu_ready", "hidden_ready", "stream_ready"))

        def after(eng, s, value):
            if not isinstance(value, int) or value > 0:
                eng.wait_ge(s, value)

        def turns(eng, slot):
            def turn(it, nominal):
                for u in range(BLOCKS):
                    for s in range(SLOTS):
                        slot(it, nominal, u, s)
            turn(0, 0)
            turn(1, 1)
            with eng.Fori(2, TURNS - BATCHES) as it:
                turn(it, 2)
            with eng.Fori(TURNS - BATCHES, TURNS - 1) as it:
                turn(it, TURNS - BATCHES)
            for last in range(TURNS - 1, TURNS + 3):
                turn(last, last)

        def in_body(nominal, u, s, lag):
            return 0 <= PER_TURN * nominal + SLOTS * u + s - lag < PER_TURN * TURNS

        def ff_turn(it, nominal, lag):
            return it - lag if 0 <= nominal - lag < TURNS else None

        def pick(tensor, index):
            if isinstance(index, int):
                return tensor[:, index, :]
            return tensor[:, bass.ds(index, 1), :].rearrange("p a n -> p (a n)")

        spare = attn_T[:, :, :].rearrange("p j t -> p (j t)")
        places = iter(np.cumsum([0, 512, 512, 128, 128, 1024, 1024]).tolist())

        def part(at, count, n):
            return spare[:, at:at + count * n].rearrange("p (a n) -> p a n", n=n)

        ctx_k = part(next(places), BATCHES, DIM)[0:XKEYS]
        ctx_v = part(next(places), BATCHES, DIM)
        mask_i = part(next(places), 1, BATCHES * XKEYS).rearrange("p a n -> p (a n)").bitcast(I32)
        logit_bias = part(next(places), BATCHES, XKEYS)
        key_diag = part(next(places), BATCHES, XHEADS * XKEYS)
        value_diag = part(next(places), 2 * BATCHES, DIM)
        xbias = sb("xbias", [P, 1])
        h_stat = sb("h_stat", [P, 8, BLOCKS])
        h_x = q_diag[:, 0, 0, 0:4, :]
        h_sq = q_diag[:, 0, 0, 4:8, :]
        h_T = q_diag[:, 0, 1, 0:4, :]
        h_logit = q_diag[:, 1, :, :, :].rearrange("p a b c -> p (a b c)")[:, 0:1024]
        h_exp = q_diag[:, 1, :, :, :].rearrange("p a b c -> p (a b c)")[:, 1024:2048]
        h_expT = rotated[:, 0:2, :].rearrange("p a b -> p (a b)")
        h_red = rotated[:, 2, 0:32]
        h_inv = rotated[:, 2, 32:64]

        def keep_q(copy, side, cs, cu):
            src = ps[side * QT:(side + 1) * QT, PS_QKT, :].rearrange("p (j t q) -> p j t q", j=4, t=2)
            dst = q_diag[side * QT:(side + 1) * QT, cu % 2, :, 4 * cs:4 * cs + 4, side * QT:(side + 1) * QT]
            return copy(dst.rearrange("p t j q -> p j t q"), src)

        def is_first_group(u, s, lag):
            return (SLOTS * u + s - lag) % PER_TURN == 0

        def keep_o(copy, side, u, s, lag):
            g = (SLOTS * u + s - lag) % PER_TURN
            tile, half = g // 2, g % 2
            src = ps[side * QT:(side + 1) * QT, PS_O, :].rearrange("p (j x q) -> p j x q", j=4, x=2)[:, :, side, :]
            return copy(attn_T[side * QT:(side + 1) * QT, 4 * half:4 * half + 4, QT * tile:QT * (tile + 1)], src)

        def rot_table(turn, n, u):
            if isinstance(turn, int):
                return rot[:, turn % 2:turn % 2 + 1, n, u, :]
            return rot[:, bass.ds(turn % 2, 1), n, u, :]

        def v_chunk(it, u, s):
            return (it if u >= 2 else it - 1), (u - 2) % BLOCKS, s // 2, s % 2

        def wqkv_piece(it, n):
            at = (it // BATCHES + 1) % 2 * (3 * INNER) + it % BATCHES * (2 * PIECE) + n * PIECE
            return slice(at, at + PIECE) if isinstance(it, int) else bass.ds(at, PIECE)

        def splits_piece(nominal, u, s):
            if nominal < TURNS - BATCHES and u >= 2 and s == 1:
                return u - 2
            return None

        block = ctx.enter_context(nc.Block())

        FF_LOADS = 16 * (1 + 3 * len(HID_PARTS) + 3)

        @block.sync
        def _(sp):
            sp.dma_start(const[:, :], consts).then_inc(const_in, 16)
            sp.dma_start(x_tok[:, :, :], x.rearrange("b (t p) c -> p (b t) c", p=P)).then_inc(x_in, 16)
            sp.dma_start(ctx_k[:, :, :], ctx_mem[:, :, 0:DIM].rearrange("b k c -> k b c")).then_inc(ctx_in, 16)
            for quad in range(4):
                sp.dma_start(ctx_v[quad * XKEYS:(quad + 1) * XKEYS, :, :],
                             ctx_mem[:, :, DIM:2 * DIM].rearrange("b k c -> k b c")).then_inc(ctx_in, 16)
            sp.dma_start(mask_i[:, :], mask.rearrange("(o b) k -> o (b k)", o=1).to_broadcast([P, BATCHES * XKEYS])
                         ).then_inc(small_in, 16)
            for dst, src in ((xbias[:, :], xb), (gates[:, 0:1], g_xattn), (gates[:, 1:2], g_ffn)):
                sp.dma_start(dst, src.rearrange("(o n) -> o n", o=1).to_broadcast([P, 1])).then_inc(small_in, 16)
            for n, src in ((0, q_scale), (2, k_scale)):
                s3 = src.rearrange("(o l) d -> o l d", o=1)
                sp.dma_start(head_scales[:, n, :, :], s3.to_broadcast([P, DEPTH, DHEAD])).then_inc(scales_in, 16)
                for h in range(2):
                    sp.dma_start(head_scales[:, n + 1, :, h * HALF:(h + 1) * HALF],
                                 s3[:, :, (1 - h) * HALF:(2 - h) * HALF].to_broadcast([P, DEPTH, HALF])
                                 ).then_inc(scales_in, 16)

            def load_pieces(row, first, count):
                for n in range(2):
                    if count > 0 or not isinstance(count, int):
                        sp.wait_ge(const_in, 16)
                        sp.wait_ge(wqkv_high_ready, count + n - 1)
                        sp.wait_ge(wqkv_low_ready, count + n - 1)
                    src = rows(wqkv, row, DIM)[:, (first + n) * PIECE:(first + n + 1) * PIECE]
                    sp.dma_start(wqkv_raw[:, n, :], src).then_inc(wqkv_in[n], 16)

            def rows(t, at, n):
                return t[at:at + n, :] if isinstance(at, int) else t[bass.ds(at, n), :]

            def load_wo(layer):
                sp.dma_start(wo_sb[:, :, :], rows(wo, layer * INNER, INNER).rearrange("(j p) c -> p j c", p=P)
                             ).then_inc(wo_in, 16)

            def load_ff(layer):
                sp.dma_start(w1_sb[:, :], rows(w1, layer * DIM, DIM)).then_inc(ff_w_in, 16)
                at = 0
                for j, m in enumerate(HID_PARTS):
                    sp.dma_start(w2_sb[0:m, j, :], rows(w2, layer * HIDDEN + at, m)).then_inc(ff_w_in, 16)
                    for part in range(2):
                        sp.dma_start(b1_sb[0:m, part, j:j + 1], rows(b1, layer * 2 * HIDDEN + part * HIDDEN + at, m)
                                     ).then_inc(ff_w_in, 16)
                    at += m
                for dst, src in ((ln_g_sb, ln_g), (ln_b_sb, ln_b), (b2_sb, b2)):
                    sp.dma_start(dst[:, :], rows(src, layer * DIM, DIM)).then_inc(ff_w_in, 16)

            load_wo(0)
            load_ff(0)
            for first in range(0, PIECES, 2):
                load_pieces(0, first, first)
            for first in range(0, PIECES, 2):
                load_pieces(DIM, first, PIECES + first)

            def next_layer(layer, wqkv_too):
                if wqkv_too:
                    load_pieces((layer + 1) * DIM, 0, PIECES * (layer + 1))
                sp.wait_ge(wo_ready, BATCHES * layer)
                load_wo(layer)
                if wqkv_too:
                    load_pieces((layer + 1) * DIM, 2, PIECES * (layer + 1) + 2)
                sp.wait_ge(w2_ready, BATCHES * layer)
                sp.wait_ge(stream_ready, BATCHES * layer)
                load_ff(layer)
                if wqkv_too:
                    for first in range(4, PIECES, 2):
                        load_pieces((layer + 1) * DIM, first, PIECES * (layer + 1) + first)

            with sp.Fori(1, DEPTH - 1) as layer:
                next_layer(layer, True)
            next_layer(DEPTH - 1, False)
            for b in range(BATCHES):
                sp.wait_ge(tail_dve, b + 1)
                sp.dma_start(out[b].rearrange("(t p) c -> p t c", p=P),
                             x_tok[:, b * BLOCKS:(b + 1) * BLOCKS, :]).then_inc(out_stored, 16)
            sp.wait_ge(out_stored, 16 * BATCHES)


        H_DVE, H_ACT, H_PE = 29, 3, 5

        @block.gpsimd
        def _(pool):
            pool.memset(minus_half[:, :], -0.5)
            pool.memset(mean_w[:, :], 1.0 / DIM)
            pool.memset(ln_eps[:, :], LN_EPS)
            pool.memset(k_T[:, :, 0:WINDOW], 0.0)
            pool.memset(shifted_high[:, 0, 0:WINDOW + 1].bitcast(F32), 0.0)
            pool.memset(shifted_low[:, 0, 0:WINDOW + 1].bitcast(F32), 0.0)
            pool.memset(ff_in[:, 0:1], 0.0).then_inc(setup_pool, 1)
            pool.wait_ge(scales_in, 16 * 6)
            pool.wait_ge(const_in, 16)

            def tables(turn):
                for n, at in enumerate((C_COS_Q, C_SIN_Q, C_COS_K, C_SIN_K)):
                    base = const[:, at:at + BLOCKS * DHEAD].rearrange("p (o u d) -> p o u d", o=1, d=DHEAD)
                    if isinstance(turn, int):
                        dst = rot[:, turn % 2:turn % 2 + 1, n, :, :]
                        scales = head_scales[:, n, turn // BATCHES:turn // BATCHES + 1, :]
                    else:
                        dst = rot[:, bass.ds(turn % 2, 1), n, :, :]
                        scales = head_scales[:, n, bass.ds(turn // BATCHES, 1), :]
                    scales = scales.rearrange("p o (u d) -> p o u d", u=1).to_broadcast([P, 1, BLOCKS, DHEAD])
                    last = pool.tensor_tensor(dst, base, scales, ALU.mult)
                last.then_inc(tables_ready, 1)

            tables(0)

            def split_low(piece, n, count):
                pool.wait_ge(wqkv_high_ready, count + 1)
                pool.tensor_tensor(wqkv_low[:, piece], wqkv_raw[:, n, :], wqkv_high[:, piece].bitcast(F32),
                                   ALU.subtract).then_inc(wqkv_low_ready, 1)

            for i in range(PIECES):
                split_low(slice(i * PIECE, (i + 1) * PIECE), i % 2, i)
            pool.wait_ge(head_dve, H_DVE * BATCHES)
            pool.wait_ge(head_pe, H_PE * BATCHES)
            pool.memset(q_diag[:, :, :, :, :], 0.0).then_inc(setup_pool, 1)

            def slot(it, nominal, u, s):
                K = PER_TURN * it + SLOTS * u + s
                if in_body(nominal, u, s, 0):
                    pool.wait_ge(floored_ready, K + 1)
                    pool.tensor_tensor(inv_norm[:, s, :], norm2_floored[:, s, :], minus_half[:, :],
                                       ALU.pow).then_inc(inv_norm_ready, 1)
                if in_body(nominal, u, s, 1):
                    c = K - 1
                    cs, cu, ct = (s - 1) % SLOTS, (u if s else (u - 1) % BLOCKS), (it if s or u else it - 1)
                    pool.wait_ge(scales_in, 16 * 6)
                    pool.wait_ge(normed_ready, c + 1)
                    after(pool, rotated_ready, c - 1)
                    pool.wait_ge(tables_ready, ct + 1)
                    src = normed[:, cs % 2, :].rearrange("p (h x d) -> p h x d", x=2, d=HALF)
                    dst = sin_part[:, cs % 2, :].rearrange("p (h x d) -> p h x d", x=2, d=HALF)
                    for h in range(2):
                        part = rot_table(ct, 1 if cs < 2 else 3, cu)[:, :, h * HALF:(h + 1) * HALF]
                        last = pool.tensor_tensor(dst[:, :, h, :], src[:, :, 1 - h, :],
                                                  part.to_broadcast([P, 8, HALF]), ALU.mult)
                    last.then_inc(sin_ready, 1)
                if in_body(nominal, u, s, 2):
                    c, cs = K - 2, (s - 2) % SLOTS
                    pool.wait_ge(sin_ready, c + 1)
                    pool.wait_ge(cos_ready, c + 1)
                    pool.tensor_tensor(rotated[:, cs, :], rotated[:, cs, :], sin_part[:, cs % 2, :],
                                       ALU.add).then_inc(rotated_ready, 1)
                n = splits_piece(nominal, u, s)
                if n is not None:
                    split_low(wqkv_piece(it, n), n, PIECES + 2 * it + n)
                if s == 3 and u == 1 and nominal + 1 < TURNS:
                    pool.wait_ge(scales_in, 16 * 6)
                    pool.wait_ge(cos_ready, PER_TURN * it)
                    tables(it + 1)

            turns(pool, slot)

        @block.scalar
        def _(act):
            act.wait_ge(small_in, 16 * 4)
            act.activation(tanh_gates[:, :], gates[:, :], ACT.Tanh).then_inc(setup_dve, 1)
            act.wait_ge(setup_pool, 1)

            def split_high(piece, n, pair):
                act.wait_ge(wqkv_in[n], 16 * (pair + 1))
                act.copy(wqkv_high[:, piece], wqkv_raw[:, n, :]).then_inc(wqkv_high_ready, 1)

            with act.Fori(0, BATCHES) as b:
                a, d = H_ACT * b, H_DVE * b
                act.wait_ge(head_dve, d + 7)
                act.activation(h_stat[:, 4, :], h_stat[:, 3, :], ACT.Sqrt, bias=ln_eps[:, :]).then_inc(head_act, 1)
                for n in range(2):
                    act.wait_ge(setup_pool, 1)
                    split_high(bass.ds((2 * b + n) * PIECE, PIECE), n, b)
                act.wait_ge(head_dve, d + 13)
                act.activation(h_exp, h_logit, ACT.Exp).then_inc(head_act, 1)
                act.wait_ge(head_dve, d + 26)
                act.activation(h_stat[:, 4, :], h_stat[:, 3, :], ACT.Sqrt, bias=ln_eps[:, :]).then_inc(head_act, 1)

            def slot(it, nominal, u, s):
                K = PER_TURN * it + SLOTS * u + s
                if in_body(nominal, u, s, 11):
                    G = K - 11
                    act.wait_ge(o_ready, G + 1)
                    if is_first_group(u, s, 11):
                        after(act, wo_ready, it)
                    keep_o(act.copy, 0, u, s, 11).then_inc(o_top_kept, 1)
                t = ff_turn(it, nominal, 2)
                if t is not None and (u, s) == (0, 3):
                    act.wait_ge(gate_kept, 3 * t + 3)
                    act.activation(gate_sb[:, :, :], gate_sb[:, :, :], ACT.Gelu).then_inc(gelu_ready, 1)
                if in_body(nominal, u, s, 0):
                    act.wait_ge(proj_ready, K + 1)
                    after(act, norm2_ready, K - 1)
                    act.activation(squares[:, s % 2, :], ps[:, s % 2, :], ACT.Square).then_inc(squares_ready, 1)
                if in_body(nominal, u, s, 8):
                    G = K - 8
                    act.wait_ge(neg_max_ready, G + 1)
                    after(act, pT_ready, G - 1)
                    for j in range(4):
                        last = act.activation(probs[:, s % 2, j, :], ps[:, PS_S, j * KT:(j + 1) * KT], ACT.Exp,
                                              bias=neg_max[:, s % 2, j:j + 1],
                                              accum_out=row_sum[:, s % 2, j:j + 1])
                    last.then_inc(exp_ready, 1)
                if in_body(nominal, u, s, 4):
                    c, cu = K - 4, (u - 1) % BLOCKS
                    act.wait_ge(qkT_ready, c + 1)
                    after(act, s_ready, c - s - 4)
                    if s == 0 and nominal <= 1:
                        act.wait_ge(setup_pool, 2)
                    if s < 2:
                        keep_q(act.copy, 0, s, cu).then_inc(q_top_ready, 1)
                    else:
                        j = s - 2
                        act.copy(k_T[:, 4 * j:4 * j + 4, WINDOW + P * cu:WINDOW + P * (cu + 1)],
                                 ps[:, PS_QKT, :].rearrange("p (j t) -> p j t", j=4)).then_inc(k_ready, 1)
                if in_body(nominal, u, s, V_LAG):
                    c = K - V_LAG
                    act.wait_ge(v_ready, c + 1)
                    after(act, o_ready, c - 3)
                    act.copy(v_tile[:, s // 2, 512 * (s % 2):512 * (s % 2) + 512],
                             ps[0:KT, PS_V, :]).then_inc(v_kept, 1)
                if in_body(nominal, u, s, 9):
                    G = K - 9
                    act.wait_ge(pT_ready, G + 1)
                    after(act, o_ready, G - 1)
                    act.copy(probs_T[:, (s - 1) % 2, :, :],
                             ps[0:KT, PS_PT, :].rearrange("p (j q) -> p j q", j=4)).then_inc(pT_kept, 1)
                n = splits_piece(nominal, u, s)
                if n is not None:
                    act.wait_ge(scales_in, 16 * 6)
                    after(act, v_ready, PER_TURN * it)
                    split_high(wqkv_piece(it, n), n, PIECES // 2 + it)
                t = ff_turn(it, nominal, 1)
                if t is not None and (u, s) == (2, 3):
                    act.wait_ge(centred, t + 1)
                    act.activation(ff_std[:, :], ff_in[:, :], ACT.Square).then_inc(ff_sq_ready, 1)
                if t is not None and (u, s) == (3, 0):
                    act.wait_ge(var_ready, t + 1)
                    after(act, ff_norm_ready, t)
                    act.activation(ff_std[:, :], ps[:, PS_FF, :], ACT.Sqrt, bias=ln_eps[:, :]).then_inc(std_ready, 1)

            turns(act, slot)

        @block.vector
        def _(dve):
            dve.wait_ge(const_in, 16)
            dve.tensor_copy(ident_bf[:, :], ident)
            dve.tensor_copy(band_bf[:, :, :], const[:, C_BAND:C_BAND + 2 * KT].rearrange("p (a k) -> p a k", a=2))
            dve.memset(gate_sb[:, :, :], 0.0)
            dve.wait_ge(small_in, 16 * 4)
            bias = logit_bias[:, :, :].rearrange("p b k -> p (b k)")
            dve.tensor_copy(bias, mask_i[:, :]).then_inc(setup_dve, 1)
            dve.wait_ge(setup_dve, 2)
            dve.tensor_scalar(bias, bias, -1.0, 1e30, ALU.add, ALU.mult).then_inc(setup_dve, 1)
            dve.wait_ge(head_pe, 1)
            head_of_row = const[:, C_HEADK:C_HEADK + XHEADS].rearrange("p (h k) -> p h k", k=1)
            for b in range(BATCHES):
                dve.tensor_tensor(key_diag[:, b, :].rearrange("p (h k) -> p h k", h=XHEADS),
                                  ps[:, 0, b * XKEYS:(b + 1) * XKEYS].rearrange("p (h k) -> p h k", h=1)
                                  .to_broadcast([P, XHEADS, XKEYS]),
                                  head_of_row.to_broadcast([P, XHEADS, XKEYS]), ALU.mult)
            dve.wait_ge(ctx_in, 16 * 5)
            for b in range(BATCHES):
                dve.tensor_tensor(value_diag[:, 2 * b:2 * b + 2, :],
                                  ctx_v[:, b:b + 1, :].to_broadcast([P, 2, DIM]),
                                  const[:, C_HEADV:C_HEADV + 2 * P].rearrange("p (a c) -> p a c", a=2), ALU.mult)
            dve.wait_ge(setup_dve, 3)
            last = dve.tensor_scalar(bias, bias, xbias[:, 0:1], None, ALU.add)
            last.then_inc(setup_dve, 1)
            dve.wait_ge(setup_dve, 4)
            dve.wait_ge(x_in, 16)

            with dve.Fori(0, BATCHES) as b:
                base, n = H_DVE * b, [0]
                tiles = x_tok[:, bass.ds(b * BLOCKS, BLOCKS), :]

                def step(ins):
                    n[0] += 1
                    ins.then_inc(head_dve, 1)
                    dve.wait_ge(head_dve, base + n[0])

                def stat(i):
                    return h_stat[:, i, :]

                def wide(ap, shape):
                    return ap.rearrange("p (a c) -> p a c", c=1).to_broadcast(shape)

                def layernorm(act_count):
                    step(dve.tensor_reduce(stat(0), h_x, AX, ALU.add))
                    step(dve.tensor_scalar(stat(1), stat(0), 1.0 / DIM, None, ALU.mult))
                    step(dve.tensor_tensor(h_x, h_x, wide(stat(1), [P, BLOCKS, DIM]), ALU.subtract))
                    step(dve.tensor_tensor(h_sq, h_x, h_x, ALU.mult))
                    step(dve.tensor_reduce(stat(2), h_sq, AX, ALU.add))
                    step(dve.tensor_scalar(stat(3), stat(2), 1.0 / DIM, None, ALU.mult))
                    dve.wait_ge(head_act, H_ACT * b + act_count)
                    step(dve.reciprocal(stat(5), stat(4)))
                    step(dve.tensor_tensor(h_x, h_x, wide(stat(5), [P, BLOCKS, DIM]), ALU.mult))

                step(dve.tensor_scalar(h_x, tiles, 1.0, None, ALU.mult))
                layernorm(1)
                dve.wait_ge(head_pe, H_PE * b + 2)
                step(dve.tensor_copy(h_T, ps[:, 1, :].rearrange("p (a c) -> p a c", c=P)))
                dve.wait_ge(head_pe, H_PE * b + 3)
                logits = ps[:, 2:4, :].rearrange("p a n -> p (a n)").rearrange("p (m k) -> p m k", k=XKEYS)
                lg = h_logit.rearrange("p (m k) -> p m k", k=XKEYS)
                ex = h_exp.rearrange("p (m k) -> p m k", k=XKEYS)
                rows32 = [P, BLOCKS * XHEADS, XKEYS]
                step(dve.scalar_tensor_tensor(lg, logits, XSCALE, logit_bias[:, bass.ds(b, 1), :].to_broadcast(rows32),
                                              ALU.mult, ALU.add))
                step(dve.tensor_reduce(h_red, lg, AX, ALU.max))
                step(dve.tensor_tensor(lg, lg, wide(h_red, rows32), ALU.subtract))
                dve.wait_ge(head_act, H_ACT * b + 2)
                step(dve.tensor_reduce(h_red, ex, AX, ALU.add))
                step(dve.reciprocal(h_inv, h_red))
                step(dve.tensor_tensor(ex, ex, wide(h_inv, rows32), ALU.mult))
                dve.wait_ge(head_pe, H_PE * b + 4)
                step(dve.tensor_copy(h_expT, ps[:, 4:6, :].rearrange("p a n -> p (a n)")))
                dve.wait_ge(head_pe, H_PE * b + 5)
                step(dve.tensor_scalar(h_x, ps[:, 6, :].rearrange("p (a c) -> p a c", c=P), tanh_gates[:, 0:1], None,
                                       ALU.mult))
                step(dve.tensor_tensor(h_x, h_x, tiles, ALU.add))
                step(dve.tensor_scalar(tiles, h_x, 1.0, None, ALU.mult))
                layernorm(3)
                dve.wait_ge(head_pe, H_PE * b + 6)
                step(dve.tensor_copy(pick(stream, b), ps[:, 7, :]))

            def shift(it, u, count):
                src = pick(stream, it % BATCHES)
                lo = P * u - (WINDOW if u else 0)
                first = 0 if u else 1
                parts = []
                for rows, late in ((slice(0, QT), 0), (slice(QT, P), 1)):
                    skip = first * late
                    at = WINDOW + P * u + skip - P * u if u == 0 else 0
                    parts.append((rows, slice(at, WINDOW + P), src[rows, lo + skip - late:P * (u + 1) - late]))
                for rows, to, block in parts:
                    last = dve.tensor_copy(shifted_high[rows, u, to], block)
                last.then_inc(high_ready, 1)
                dve.wait_ge(high_ready, count)
                for rows, to, block in parts:
                    last = dve.tensor_tensor(shifted_low[rows, u, to], block, shifted_high[rows, u, to].bitcast(F32),
                                             ALU.subtract)
                last.then_inc(shifted_ready, 1)

            shift(0, 0, 1)
            shift(0, 1, 2)

            def slot(it, nominal, u, s):
                K = PER_TURN * it + SLOTS * u + s
                t1, t2 = ff_turn(it, nominal, 1), ff_turn(it, nominal, 2)
                if in_body(nominal, u, s, 9):
                    G, r = K - 9, (s - 1) % 2
                    dve.wait_ge(inv_sum_ready, G + 1)
                    dve.tensor_tensor(probs[:, r, :, :], probs[:, r, :, :],
                                      inv_sum[:, r, :].rearrange("p (j k) -> p j k", k=1).to_broadcast([P, 4, KT]),
                                      ALU.mult).then_inc(probs_ready, 1)
                if t2 is not None and (u, s) == (1, 2):
                    hidden(t2, 1)
                if in_body(nominal, u, s, 8):
                    G = K - 8
                    dve.wait_ge(s_ready, G + 1)
                    scores = ps[:, PS_S, 0:4 * KT].rearrange("p (j k) -> p j k", j=4)
                    dve.tensor_reduce(neg_max[:, s % 2, :], scores, AX, ALU.max, negate=True).then_inc(neg_max_ready, 1)
                if in_body(nominal, u, s, 2):
                    c, cs = K - 2, (s - 2) % SLOTS
                    cu, ct = (u if s > 1 else (u - 1) % BLOCKS), (it if s > 1 or u else it - 1)
                    dve.wait_ge(normed_ready, c + 1)
                    dve.wait_ge(tables_ready, ct + 1)
                    after(dve, qkT_ready, c - 3)
                    dve.tensor_tensor(rotated[:, cs, :].rearrange("p (h d) -> p h d", h=8),
                                      normed[:, cs % 2, :].rearrange("p (h d) -> p h d", h=8),
                                      rot_table(ct, 0 if cs < 2 else 2, cu).to_broadcast([P, 8, DHEAD]),
                                      ALU.mult).then_inc(cos_ready, 1)
                if in_body(nominal, u, s, 1):
                    c, cs = K - 1, (s - 1) % SLOTS
                    dve.wait_ge(inv_norm_ready, c + 1)
                    after(dve, sin_ready, c - 1)
                    dve.tensor_tensor(normed[:, cs % 2, :].rearrange("p (h d) -> p h d", h=8),
                                      ps[:, cs % 2, :].rearrange("p (h d) -> p h d", h=8),
                                      inv_norm[:, cs, :].rearrange("p (h d) -> p h d", d=1)
                                      .to_broadcast([P, 8, DHEAD]), ALU.mult).then_inc(normed_ready, 1)
                if t1 is not None and (u, s) == (3, 1):
                    dve.wait_ge(std_ready, t1 + 1)
                    dve.reciprocal(ff_std[:, :], ff_std[:, :]).then_inc(ff_dve, 1)
                if in_body(nominal, u, s, 0):
                    dve.wait_ge(squares_ready, K + 1)
                    dve.tensor_reduce(norm2[:, s, :], squares[:, s % 2, :].rearrange("p (h d) -> p h d", h=8), AX,
                                      ALU.add).then_inc(norm2_ready, 1)
                if t1 is not None and (u, s) == (2, 2):
                    dve.wait_ge(wo_ready, t1 + 1)
                    dve.tensor_tensor(mid[:, :], ps[:, PS_FF, :], pick(stream, t1 % BATCHES), ALU.add
                                      ).then_inc(mid_ready, 1)
                if t1 is not None and (u, s) == (2, 3):
                    dve.wait_ge(mean_ready, t1 + 1)
                    dve.tensor_tensor(ff_in[:, :], ff_in[:, :], ps[:, PS_FF, :], ALU.subtract).then_inc(centred, 1)
                if t1 is not None and (u, s) == (3, 1):
                    dve.wait_ge(ff_dve, 2 * t1 + 1)
                    dve.wait_ge(ff_w_in, FF_LOADS * (t1 // BATCHES + 1))
                    dve.scalar_tensor_tensor(ff_in[:, :], ff_in[:, :], ln_g_sb[:, 0:1], ff_std[:, :],
                                             ALU.mult, ALU.mult).then_inc(ff_dve, 1)
                if t1 is not None and (u, s) == (3, 2):
                    dve.wait_ge(ff_dve, 2 * t1 + 2)
                    dve.tensor_scalar(ff_in[:, :], ff_in[:, :], ln_b_sb[:, 0:1], None, ALU.add
                                      ).then_inc(ff_norm_ready, 1)
                if t2 is not None and (u, s) == (0, 3):
                    hidden(t2, 0)
                if s == 3 and nominal * BLOCKS + u + 2 < TURNS * BLOCKS:
                    after(dve, v_ready, K - 7)
                    shift(it if u < 2 else it + 1, (u + 2) % BLOCKS, BLOCKS * it + u + 3)
                if in_body(nominal, u, s, 0):
                    dve.wait_ge(norm2_ready, K + 1)
                    dve.tensor_scalar(norm2_floored[:, s, :], norm2[:, s, :], NORM_FLOOR ** 2, None,
                                      ALU.max).then_inc(floored_ready, 1)
                if t1 is not None and (u, s) == (2, 2):
                    dve.wait_ge(mid_ready, t1 + 1)
                    dve.tensor_copy(ff_in[0:QT, :], mid[0:QT, :])
                    dve.memset(ff_in[QT:P, 0:1], 0.0)
                    dve.tensor_copy(ff_in[QT:P, 1:TOKENS], mid[QT:P, 0:TOKENS - 1]).then_inc(ff_in_ready, 1)
                if t2 is not None and (u, s) == (2, 0):
                    dve.wait_ge(w2_ready, t2 + 1)
                    dve.scalar_tensor_tensor(pick(stream, t2 % BATCHES), ps[:, PS_FF, :], b2_sb[:, 0:1], mid[:, :],
                                             ALU.add, ALU.add).then_inc(stream_ready, 1)
                if in_body(nominal, u, s, 8):
                    G, r = K - 8, s % 2
                    dve.wait_ge(exp_ready, G + 1)
                    dve.reciprocal(inv_sum[:, r, :], row_sum[:, r, :]).then_inc(inv_sum_ready, 1)
                if t1 is not None and (u, s) == (3, 3):
                    gate(t1, 0)
                if t2 is not None and (u, s) in ((0, 0), (0, 2)):
                    gate(t2, 1 + s // 2)
                if t2 is not None and (u, s) == (1, 2):
                    hidden(t2, 2)
                if in_body(nominal, u, s, 4) and s < 2:
                    c = K - 4
                    dve.wait_ge(qkT_ready, c + 1)
                    after(dve, s_ready, c - s - 4)
                    if s == 0 and nominal <= 1:
                        dve.wait_ge(setup_pool, 2)
                    keep_q(dve.tensor_copy, 1, s, (u - 1) % BLOCKS).then_inc(q_low_ready, 1)
                if in_body(nominal, u, s, 10):
                    G = K - 10
                    dve.wait_ge(o_ready, G + 1)
                    if is_first_group(u, s, 10):
                        after(dve, wo_ready, it)
                    keep_o(dve.tensor_copy, 1, u, s, 10).then_inc(o_low_kept, 1)

            def gate(t, j):
                m = HID_PARTS[j]
                dve.wait_ge(gate_ready, 3 * t + j + 1)
                after(dve, w2_ready, t)
                dve.tensor_scalar(gate_sb[0:m, j, :], ps[0:m, PS_FF, :], b1_sb[0:m, 1, j:j + 1], None, ALU.add
                                  ).then_inc(gate_kept, 1)

            def hidden(t, j):
                m = HID_PARTS[j]
                dve.wait_ge(lin_ready, 3 * t + j + 1)
                dve.wait_ge(gelu_ready, t + 1)
                dve.scalar_tensor_tensor(gate_sb[0:m, j, :], ps[0:m, PS_FF, :], b1_sb[0:m, 0, j:j + 1],
                                         gate_sb[0:m, j, :], ALU.add, ALU.mult).then_inc(hidden_ready, 1)

            turns(dve, slot)

            for b in range(BATCHES):
                tiles = x_tok[:, b * BLOCKS:(b + 1) * BLOCKS, :]
                dve.wait_ge(tail_pe, b + 1)
                dve.scalar_tensor_tensor(tiles, ps[:, b, :].rearrange("p (t c) -> p t c", c=DIM),
                                         tanh_gates[:, 1:2], tiles, ALU.mult, ALU.add).then_inc(tail_dve, 1)

        @block.tensor
        def _(pe):
            pe.wait_ge(const_in, 16)
            pe.wait_ge(ctx_in, 16 * 5)
            for b in range(BATCHES):
                last = nc.tensor.transpose(ps[:, 0, b * XKEYS:(b + 1) * XKEYS], ctx_k[:, b, :], ident[0:XKEYS, 0:XKEYS])
            last.then_inc(head_pe, 1)
            pe.wait_ge(setup_dve, 4)
            with pe.Fori(0, BATCHES) as b:
                def transposed(bank, src):
                    for i in range(BLOCKS):
                        last = nc.tensor.transpose(ps[:, bank, i * P:(i + 1) * P], src[:, i, :], ident)
                    return last

                d = H_DVE * b
                pe.wait_ge(head_dve, d + 9)
                transposed(1, h_x).then_inc(head_pe, 1)
                pe.wait_ge(head_dve, d + 10)
                for i in range(BLOCKS):
                    last = nc.tensor.matmul(ps[:, 2 + i // 2, 256 * (i % 2):256 * (i % 2) + 256], h_T[:, i, :],
                                            pick(key_diag, b), start=True, stop=True)
                last.then_inc(head_pe, 1)
                pe.wait_ge(head_dve, d + 16)
                for i in range(2 * BLOCKS):
                    last = nc.tensor.transpose(ps[:, 4 + i // 4, P * (i % 4):P * (i % 4) + P],
                                               h_exp[:, P * i:P * (i + 1)], ident)
                last.then_inc(head_pe, 1)
                pe.wait_ge(head_dve, d + 17)
                for i in range(BLOCKS):
                    for j in range(2):
                        last = nc.tensor.matmul(ps[:, 6, P * i:P * (i + 1)], h_expT[:, P * (2 * i + j):P * (2 * i + j + 1)],
                                                pick(value_diag, 2 * b + j), start=(j == 0), stop=(j == 1))
                last.then_inc(head_pe, 1)
                pe.wait_ge(head_dve, d + 28)
                transposed(7, h_x).then_inc(head_pe, 1)

            pe.wait_ge(head_dve, H_DVE * BATCHES)
            pe.wait_ge(setup_pool, 1)

            def slot(it, nominal, u, s):
                K = PER_TURN * it + SLOTS * u + s
                half = s % 2
                if in_body(nominal, u, s, 0):
                    pe.wait_ge(wqkv_high_ready, PIECES * (it // BATCHES + 1))
                    pe.wait_ge(wqkv_low_ready, PIECES * (it // BATCHES + 1))
                    pe.wait_ge(shifted_ready, BLOCKS * it + u + 1)
                    after(pe, normed_ready, K - 1)
                    project(ps[:, s % 2, :], u, slice(WINDOW, WINDOW + P), it, 512 * s).then_inc(proj_ready, 1)
                if in_body(nominal, u, s, 8):
                    G = K - 8
                    gu = (u - 2) % BLOCKS
                    pe.wait_ge(q_top_ready, 2 * (BLOCKS * it + u - 2) + half + 1)
                    pe.wait_ge(q_low_ready, 2 * (BLOCKS * it + u - 2) + half + 1)
                    pe.wait_ge(k_ready, 2 * (BLOCKS * it + u - 2) + half + 1)
                    after(pe, exp_ready, G)
                    first = 0 if gu == 0 and s < 2 else 1
                    nc.tensor.matmul(ps[:, PS_S, 0:4 * KT].rearrange("p (j k) -> p j k", j=4), ident_bf[:, :],
                                     band_bf[:, first:first + 1, :].to_broadcast([P, 4, KT]), start=True, stop=False,
                                     skip_group_check=True)
                    t0 = P * gu + QT * (s // 2)
                    for j in range(4):
                        pair = 4 * half + j
                        last = nc.tensor.matmul(ps[:, PS_S, j * KT:(j + 1) * KT], q_diag[:, gu % 2, s // 2, pair, :],
                                                k_T[:, pair, t0:t0 + KT], start=False, stop=(j == 3),
                                                skip_group_check=True)
                    last.then_inc(s_ready, 1)
                if in_body(nominal, u, s, V_LAG):
                    after(pe, v_kept, K - V_LAG)
                    vt, vu, tile, _ = v_chunk(it, u, s)
                    project(ps[0:KT, PS_V, :], vu, slice(QT * tile, QT * tile + KT), vt, 2 * INNER + 512 * half
                            ).then_inc(v_ready, 1)
                if in_body(nominal, u, s, 4):
                    c = K - 4
                    pe.wait_ge(rotated_ready, c + 1)
                    blocks_before = BLOCKS * it + u - 1
                    if s < 3:
                        after(pe, q_top_ready, 2 * blocks_before + min(s, 2))
                        after(pe, q_low_ready, 2 * blocks_before + min(s, 2))
                    after(pe, k_ready, 2 * blocks_before + max(s - 2, 0))
                    for j in range(4):
                        last = nc.tensor.transpose(ps[:, PS_QKT, P * j:P * (j + 1)],
                                                   rotated[:, s, P * j:P * (j + 1)], ident)
                    last.then_inc(qkT_ready, 1)
                feed_forward(it, nominal, u, s)
                if in_body(nominal, u, s, 9):
                    G = K - 9
                    pe.wait_ge(probs_ready, G + 1)
                    after(pe, pT_kept, G)
                    for j in range(4):
                        last = nc.tensor.transpose(ps[0:KT, PS_PT, P * j:P * (j + 1)], probs[:, (s - 1) % 2, j, :], ident)
                    last.then_inc(pT_ready, 1)
                if in_body(nominal, u, s, 10):
                    G = K - 10
                    g = (SLOTS * u + s - 10) % PER_TURN
                    pe.wait_ge(pT_kept, G + 1)
                    after(pe, o_top_kept, G)
                    after(pe, o_low_kept, G)
                    pe.wait_ge(v_kept, G + 1)
                    for j in range(4):
                        pair = 4 * (g % 2) + j
                        last = nc.tensor.matmul(ps[:, PS_O, P * j:P * (j + 1)], v_tile[:, g // 2 % 2, P * pair:P * (pair + 1)],
                                                probs_T[:, s % 2, j, :], start=True, stop=True)
                    last.then_inc(o_ready, 1)

            def project(out, u, tokens, it, at):
                for n, (x_part, w_part) in enumerate(((shifted_low, wqkv_high), (shifted_high, wqkv_low),
                                                      (shifted_high, wqkv_high))):
                    col = it // BATCHES % 2 * (3 * INNER) + at
                    w = w_part[:, col:col + 512] if isinstance(it, int) else w_part[:, bass.ds(col, 512)]
                    last = nc.tensor.matmul(out, x_part[:, u, tokens], w, start=(n == 0), stop=(n == 2))
                return last

            def feed_forward(it, nominal, u, s):
                bank = ps[:, PS_FF, :]
                t = ff_turn(it, nominal, 1)
                if t is not None and (u, s) in ((2, 1), (2, 2)):
                    part = s - 1
                    if part == 0:
                        pe.wait_ge(wo_in, 16 * (t // BATCHES + 1))
                        after(pe, stream_ready, t)
                    pe.wait_ge(o_top_kept, PER_TURN * t + 15 + part)
                    pe.wait_ge(o_low_kept, PER_TURN * t + 15 + part)
                    for j in range(4 * part, 4 * part + 4):
                        last = nc.tensor.matmul(bank, wo_sb[:, j, :], attn_T[:, j, :], start=(j == 0),
                                                stop=(j == PAIRS - 1))
                    if part == 1:
                        last.then_inc(wo_ready, 1)
                if t is not None and (u, s) == (2, 3):
                    pe.wait_ge(ff_in_ready, t + 1)
                    nc.tensor.matmul(bank, mean_w[:, :], ff_in[:, :], start=True, stop=True).then_inc(mean_ready, 1)
                if t is not None and (u, s) == (3, 0):
                    pe.wait_ge(ff_sq_ready, t + 1)
                    nc.tensor.matmul(bank, mean_w[:, :], ff_std[:, :], start=True, stop=True).then_inc(var_ready, 1)
                if t is not None and (u, s) == (3, 3):
                    gate_or_lin(t, 0, HIDDEN, gate_kept, 3 * t, gate_ready)
                t = ff_turn(it, nominal, 2)
                if t is None:
                    return
                if (u, s) in ((0, 0), (0, 2)):
                    j = 1 + s // 2
                    gate_or_lin(t, j, HIDDEN, gate_kept, 3 * t + j, gate_ready)
                if (u, s) == (0, 3):
                    gate_or_lin(t, 0, 0, gate_kept, 3 * t + 3, lin_ready)
                if (u, s) in ((1, 0), (1, 2)):
                    j = 1 + s // 2
                    gate_or_lin(t, j, 0, hidden_ready, 3 * t + j, lin_ready)
                if (u, s) == (2, 0):
                    pe.wait_ge(hidden_ready, 3 * t + 3)
                    for j, m in enumerate(HID_PARTS):
                        last = nc.tensor.matmul(bank, w2_sb[0:m, j, :], gate_sb[0:m, j, :], start=(j == 0), stop=(j == 2))
                    last.then_inc(w2_ready, 1)

            def gate_or_lin(t, j, col, left, count, ready):
                m, col = HID_PARTS[j], col + sum(HID_PARTS[:j])
                pe.wait_ge(ff_norm_ready, t + 1)
                pe.wait_ge(ff_w_in, FF_LOADS * (t // BATCHES + 1))
                after(pe, left, count)
                nc.tensor.matmul(ps[0:m, PS_FF, :], w1_sb[:, col:col + m], ff_in[:, :], start=True, stop=True
                                 ).then_inc(ready, 1)

            turns(pe, slot)

            pe.wait_ge(stream_ready, TURNS)
            for b in range(BATCHES):
                for i in range(BLOCKS):
                    last = nc.tensor.transpose(ps[:, b, i * P:(i + 1) * P], stream[:, b, i * P:(i + 1) * P], ident)
                last.then_inc(tail_pe, 1)


_INS = ['x', 'ctx_2048', 'mask_BxS2_ik0', 'g_xattn', 'g_ffn', 'L0_xattn_b', 'L0_ffn_Wqkv', 'L0_ffn_q_scale',
        'L0_ffn_k_scale', 'L0_ffn_Wo', 'L0_ffn_ln_g', 'L0_ffn_ln_b', 'L0_ffn_W1', 'L0_ffn_b1', 'L0_ffn_W2',
        'L0_ffn_b2']
_SHAPES = {'L0_ffn_Wqkv': (DEPTH * DIM, 3 * INNER), 'L0_ffn_Wo': (DEPTH * INNER, DIM),
           'L0_ffn_W1': (DEPTH * DIM, 2 * HIDDEN), 'L0_ffn_W2': (DEPTH * HIDDEN, DIM),
           'L0_ffn_ln_g': (DEPTH * DIM, 1), 'L0_ffn_ln_b': (DEPTH * DIM, 1), 'L0_ffn_b2': (DEPTH * DIM, 1),
           'L0_ffn_b1': (DEPTH * 2 * HIDDEN, 1)}


def kernel(**inputs):
    import numpy as _np
    import concourse.bacc as _bacc
    from concourse import mybir as _mybir
    from concourse.bass_utils import run_bass_kernel_spmd as _run

    nc = _bacc.Bacc("TRN2", target_bir_lowering=False, num_devices=1)
    arrays, args = {}, []
    for name in _INS:
        a = _np.ascontiguousarray(inputs[name])
        a = a.reshape(_SHAPES.get(name, a.shape))
        arrays[f"in_{name}_dram"] = a
        args.append(nc.dram_tensor(f"in_{name}_dram", a.shape, _mybir.dt.from_np(a.dtype), kind="ExternalInput").ap())
    arrays["consts_dram"] = shape_constants()
    args.append(nc.dram_tensor("consts_dram", (P, C_END), F32, kind="ExternalInput").ap())
    args.append(nc.dram_tensor("out_dram", (BATCHES, TOKENS, DIM), F32, kind="ExternalOutput").ap())
    build(nc, *args)
    r = _run(nc, [arrays], core_ids=[0])
    return r.results[0]["out_dram"]
```

```python
from contextlib import ExitStack

import numpy as np

import concourse.bass as bass
from concourse import mybir

F32 = mybir.dt.float32
BF16 = mybir.dt.bfloat16
F32R = mybir.dt.float32r
I32 = mybir.dt.int32
ALU = mybir.AluOpType
ACT = mybir.ActivationFunctionType
AX = mybir.AxisListType.X

P = 128
BATCHES, TOKENS, DIM = 4, 512, 128
DEPTH, HEADS, DHEAD, WINDOW = 6, 16, 64, 32
HALF = DHEAD // 2
INNER = HEADS * DHEAD
HIDDEN = int(DIM * 4 * 2 / 3)
QK_SCALE = 8.0
NORM_FLOOR = 1e-12
LN_EPS = 1e-5
BLOCKS = TOKENS // P
SLOTS = 4
PAIRS = HEADS // 2
QT = 64
KT = QT + WINDOW
TURNS = DEPTH * BATCHES
PER_TURN = BLOCKS * SLOTS
HID_PARTS = (114, 114, 113)
HID_MAX = 114
MASKED = -float(2 ** 100)
PIECES = 8
PIECE = 3 * INNER // PIECES
XHEADS, XKEYS = 8, 32
XDEPTH = DIM // XHEADS
XSCALE = float(XDEPTH) ** -0.5

C_IDENT = 0
C_COS_Q = C_IDENT + P
C_SIN_Q = C_COS_Q + BLOCKS * DHEAD
C_COS_K = C_SIN_Q + BLOCKS * DHEAD
C_SIN_K = C_COS_K + BLOCKS * DHEAD
C_BODY = C_SIN_K + BLOCKS * DHEAD
C_BAND = C_BODY
C_HEADK = C_BAND + 2 * KT
C_HEADV = C_HEADK + XHEADS
C_END = C_HEADV + 2 * P


def shape_constants():
    c = np.zeros((P, C_END), np.float32)
    row = np.arange(P)[:, None]
    c[:, C_IDENT:C_IDENT + P] = np.eye(P)
    key = np.arange(KT)[None, :]
    query = row % QT
    seen = (key >= query) & (key <= query + WINDOW)
    c[:, C_BAND:C_BAND + KT] = np.where(seen & (key >= WINDOW), 0.0, MASKED)
    c[:, C_BAND + KT:C_BAND + 2 * KT] = np.where(seen, 0.0, MASKED)
    c[:, C_HEADK:C_HEADK + XHEADS] = row // XDEPTH == np.arange(XHEADS)[None, :]
    for j in range(2):
        c[:, C_HEADV + j * P:C_HEADV + (j + 1) * P] = row // XKEYS + 4 * j == np.arange(P)[None, :] // XDEPTH
    half = np.arange(0, DHEAD, 2, dtype=np.float32)
    inv_freq = (1.0 / 10000.0 ** (half.astype(np.float64) / DHEAD)).astype(np.float32)
    t = np.arange(TOKENS, dtype=np.float32)
    freqs = (t[:, None] * inv_freq[None, :]).astype(np.float32).astype(np.float64)
    base = (half.astype(np.float64) + 0.4 * DHEAD) / (1.4 * DHEAD)
    power = (t.astype(np.float64) - TOKENS // 2) / (WINDOW // 2)
    scale = base[None, :] ** power[:, None]
    sign = np.concatenate([-np.ones(HALF), np.ones(HALF)])
    for at_cos, at_sin, s in ((C_COS_Q, C_SIN_Q, QK_SCALE * scale), (C_COS_K, C_SIN_K, 1.0 / scale)):
        cos = np.tile(np.cos(freqs) * s, 2)
        sin = np.tile(np.sin(freqs) * s, 2) * sign
        for at, table in ((at_cos, cos), (at_sin, sin)):
            c[:, at:at + BLOCKS * DHEAD] = table.reshape(BLOCKS, P, DHEAD).transpose(1, 0, 2).reshape(P, -1)
    return c


def build(nc, x, ctx_mem, mask, g_xattn, g_ffn, xb, wqkv, q_scale, k_scale, wo, ln_g, ln_b, w1, b1, w2, b2,
          consts, out):
    ctx = ExitStack()
    with ctx:
        def sb(name, shape, dt=F32):
            return ctx.enter_context(nc.sbuf_tensor(name, shape, dt))

        def sem(name):
            return ctx.enter_context(nc.semaphore(name))

        const = sb("const", [P, C_BODY])
        ident = const[:, C_IDENT:C_IDENT + P]
        ident_bf = sb("ident_bf", [P, P], BF16)
        band_bf = sb("band_bf", [P, 2, KT], BF16)
        mean_w = sb("mean_w", [P, P])
        ln_eps = sb("ln_eps", [P, 1])
        minus_half = sb("minus_half", [P, 8])
        gates = sb("gates", [P, 2])
        tanh_gates = sb("tanh_gates", [P, 2])
        x_tok = sb("x_tok", [P, BATCHES * BLOCKS, DIM])
        stream = sb("stream", [P, BATCHES, TOKENS])
        wqkv_high = sb("wqkv_high", [P, 2 * 3 * INNER], F32R)
        wqkv_low = sb("wqkv_low", [P, 2 * 3 * INNER], F32R)
        wqkv_raw = sb("wqkv_raw", [P, 2, PIECE])
        wo_sb = sb("wo_sb", [P, PAIRS, DIM])
        w1_sb = sb("w1_sb", [P, 2 * HIDDEN])
        w2_sb = sb("w2_sb", [HID_MAX, 3, DIM])
        ln_g_sb = sb("ln_g_sb", [P, 1])
        ln_b_sb = sb("ln_b_sb", [P, 1])
        b2_sb = sb("b2_sb", [P, 1])
        b1_sb = sb("b1_sb", [HID_MAX, 2, 3])
        head_scales = sb("head_scales", [P, 2, DEPTH, DHEAD])
        rot = sb("rot", [P, 2, 4, BLOCKS, DHEAD])
        shifted_high = sb("shifted_high", [P, BLOCKS, WINDOW + P], F32R)
        shifted_low = sb("shifted_low", [P, BLOCKS, WINDOW + P], F32R)
        squares = sb("squares", [P, 2, 512])
        norm2 = sb("norm2", [P, 4, 8])
        norm2_floored = sb("norm2_floored", [P, 4, 8])
        inv_norm = sb("inv_norm", [P, 4, 8])
        normed = sb("normed", [P, 2, 512])
        sin_part = sb("sin_part", [P, 2, 512])
        rotated = sb("rotated", [P, 4, 512])
        q_diag = sb("q_diag", [P, 2, 2, PAIRS, P])
        k_T = sb("k_T", [P, PAIRS, WINDOW + TOKENS])
        v_first = sb("v_first", [P, 2, INNER])
        v_last = sb("v_last", [P, 2, INNER])
        neg_max = sb("neg_max", [P, 2, 4])
        row_sum = sb("row_sum", [P, 2, 4])
        inv_sum = sb("inv_sum", [P, 2, 4])
        exps = sb("exps", [P, 2, 4, P])
        probs = sb("probs", [P, 2, 4, P])
        probs_T = sb("probs_T", [P, 2, 4, P])
        attn_T = sb("attn_T", [P, PAIRS, TOKENS])
        mid = sb("mid", [P, TOKENS])
        ff_in = sb("ff_in", [P, TOKENS])
        ff_std = sb("ff_std", [P, TOKENS])
        gate_sb = sb("gate_sb", [HID_MAX, 3, TOKENS])

        ps = ctx.enter_context(nc.psum_tensor("ps", [P, 8, 512], F32))
        PS_V, PS_QKT, PS_S, PS_PT, PS_O, PS_FF = 2, 3, 4, 5, 6, 7

        start_const_in = sem("start_const_in")
        const_in, x_in, ctx_in, small_in, scales_in = (sem(n) for n in ("const_in", "x_in", "ctx_in", "small_in",
                                                                        "scales_in"))
        wqkv_in = [sem("wqkv_first_in"), sem("wqkv_second_in")]
        wo_in, ff_w_in, out_stored = (sem(n) for n in ("wo_in", "ff_w_in", "out_stored"))
        setup_dve, setup_pool = sem("setup_dve"), sem("setup_pool")
        ctxT_ready, sums_ready, means_ready, x_centred, x_squared, var_sums_ready, x_std_ready, x_inv_ready = (
            sem(n) for n in ("ctxT_ready", "sums_ready", "means_ready", "x_centred", "x_squared", "var_sums_ready",
                             "x_std_ready", "x_inv_ready"))
        x_normed, xT_ready, xT_kept, logits_ready, logits_biased, logits_max_ready, logits_less_max = (
            sem(n) for n in ("x_normed", "xT_ready", "xT_kept", "logits_ready", "logits_biased", "logits_max_ready",
                             "logits_less_max"))
        x_exp_ready, exp_sums_ready, inv_sums_ready, x_probs_ready, x_probsT_ready, x_probsT_kept = (
            sem(n) for n in ("x_exp_ready", "exp_sums_ready", "inv_sums_ready", "x_probs_ready", "x_probsT_ready",
                             "x_probsT_kept"))
        attended_ready, residual_ready, streamT_ready, stream_kept = (
            sem(n) for n in ("attended_ready", "residual_ready", "streamT_ready", "stream_kept"))
        tail_pe, tail_dve = sem("tail_pe"), sem("tail_dve")
        tables_ready, high_ready, shifted_ready = sem("tables_ready"), sem("high_ready"), sem("shifted_ready")
        wqkv_high_ready, wqkv_low_ready = sem("wqkv_high_ready"), sem("wqkv_low_ready")
        proj_ready, v_ready, qkT_ready, s_ready, pT_ready, o_ready = (
            sem(n) for n in ("proj_ready", "v_ready", "qkT_ready", "s_ready", "pT_ready", "o_ready"))
        squares_ready, norm2_ready, floored_ready, inv_norm_ready, normed_ready = (
            sem(n) for n in ("squares_ready", "norm2_ready", "floored_ready", "inv_norm_ready", "normed_ready"))
        cos_ready, sin_ready, rotated_ready = sem("cos_ready"), sem("sin_ready"), sem("rotated_ready")
        q_top_ready, q_low_ready, k_ready, v_first_kept, v_last_kept, v_before_kept = (
            sem(n) for n in ("q_top_ready", "q_low_ready", "k_ready", "v_first_kept", "v_last_kept", "v_before_kept"))
        neg_max_ready, exp_ready, inv_sum_ready, probs_ready, pT_kept = (
            sem(n) for n in ("neg_max_ready", "exp_ready", "inv_sum_ready", "probs_ready", "pT_kept"))
        o_top_kept, o_low_kept = sem("o_top_kept"), sem("o_low_kept")
        wo_ready, mean_ready, var_ready, gate_ready, lin_ready, w2_ready = (
            sem(n) for n in ("wo_ready", "mean_ready", "var_ready", "gate_ready", "lin_ready", "w2_ready"))
        mid_ready, ff_in_ready, centred, ff_sq_ready, std_ready, inv_std_ready, scaled_ready = (
            sem(n) for n in ("mid_ready", "ff_in_ready", "centred", "ff_sq_ready", "std_ready", "inv_std_ready",
                             "scaled_ready"))
        ff_norm_ready, gate_kept, gelu_ready, hidden_ready, stream_ready = (
            sem(n) for n in ("ff_norm_ready", "gate_kept", "gelu_ready", "hidden_ready", "stream_ready"))

        def after(eng, s, value):
            if not isinstance(value, int) or value > 0:
                eng.wait_ge(s, value)

        def turns(eng, slot):
            def turn(it, nominal):
                for u in range(BLOCKS):
                    for s in range(SLOTS):
                        slot(it, nominal, u, s)
            turn(0, 0)
            turn(1, 1)
            with eng.Fori(2, TURNS - BATCHES) as it:
                turn(it, 2)
            with eng.Fori(TURNS - BATCHES, TURNS - 1) as it:
                turn(it, TURNS - BATCHES)
            for last in range(TURNS - 1, TURNS + 3):
                turn(last, last)

        def in_body(nominal, u, s, lag):
            return 0 <= PER_TURN * nominal + SLOTS * u + s - lag < PER_TURN * TURNS

        def ff_turn(it, nominal, lag):
            return it - lag if 0 <= nominal - lag < TURNS else None

        def pick(tensor, index):
            if isinstance(index, int):
                return tensor[:, index, :]
            return tensor[:, bass.ds(index, 1), :].rearrange("p a n -> p (a n)")

        spare = attn_T[:, :, :].rearrange("p j t -> p (j t)")
        places = iter(np.cumsum([0, 512, 512, 128, 128, 1024, 1024, C_END - C_BODY]).tolist())

        def part(at, count, n):
            return spare[:, at:at + count * n].rearrange("p (a n) -> p a n", n=n)

        ctx_k = part(next(places), BATCHES, DIM)[0:XKEYS]
        ctx_v = part(next(places), BATCHES, DIM)
        mask_i = part(next(places), 1, BATCHES * XKEYS).rearrange("p a n -> p (a n)").bitcast(I32)
        logit_bias = part(next(places), BATCHES, XKEYS)
        key_diag = part(next(places), BATCHES, XHEADS * XKEYS)
        value_diag = part(next(places), 2 * BATCHES, DIM)
        start_const = part(next(places), 1, C_END - C_BODY).rearrange("p a n -> p (a n)")
        band = start_const[:, 0:2 * KT]
        head_of_channel = start_const[:, C_HEADK - C_BODY:C_HEADK - C_BODY + XHEADS]
        head_of_key = start_const[:, C_HEADV - C_BODY:C_HEADV - C_BODY + 2 * P]
        xbias = sb("xbias", [P, 1])
        h_stat = sb("h_stat", [P, 5, BATCHES, BLOCKS])
        q_place = q_diag[:, :, :, :, :].rearrange("p a b c d -> p (a b c d)")
        k_place = k_T[:, :, :].rearrange("p j t -> p (j t)")
        rotated_place = rotated[:, :, :].rearrange("p a n -> p (a n)")
        h_x = [flat[:, at:at + TOKENS].rearrange("p (a c) -> p a c", c=P) for flat, at in (
            (q_place, 0), (normed[:, 0, :], 0), (k_place, 0), (sin_part[:, 0, :], 0))]
        h_T = [flat[:, at:at + TOKENS].rearrange("p (a c) -> p a c", c=P) for flat, at in (
            (q_place, 512), (normed[:, 1, :], 0), (k_place, 512), (sin_part[:, 1, :], 0))]
        h_logit = [flat[:, at:at + 1024] for flat, at in (
            (q_place, 1024), (rotated_place, 0), (k_place, 1024), (q_place, 3072))]
        h_expT = [flat[:, at:at + 1024] for flat, at in (
            (q_place, 2048), (rotated_place, 1024), (k_place, 2048), (k_place, 3072))]
        h_red = squares[:, 0, 0:BATCHES * 32].rearrange("p (b n) -> p b n", b=BATCHES)
        h_inv = squares[:, 0, P:P + BATCHES * 32].rearrange("p (b n) -> p b n", b=BATCHES)

        def keep_q(copy, side, cs, cu):
            src = ps[side * QT:(side + 1) * QT, PS_QKT, :].rearrange("p (j t q) -> p j t q", j=4, t=2)
            dst = q_diag[side * QT:(side + 1) * QT, cu % 2, :, 4 * cs:4 * cs + 4, side * QT:(side + 1) * QT]
            return copy(dst.rearrange("p t j q -> p j t q"), src)

        def ends(t):
            return isinstance(t, int) and t == TURNS - 1

        def gate_bank(t, j):
            return (PS_FF, PS_S, PS_PT)[j] if ends(t) else PS_FF

        def lin_bank(t, j):
            return (PS_O, PS_FF, PS_S)[j] if ends(t) else PS_FF

        def w2_bank(t):
            return PS_PT if ends(t) else PS_FF

        def is_first_group(u, s, lag):
            return (SLOTS * u + s - lag) % PER_TURN == 0

        def keep_o(copy, side, u, s, lag):
            g = (SLOTS * u + s - lag) % PER_TURN
            tile, half = g // 2, g % 2
            src = ps[side * QT:(side + 1) * QT, PS_O, :].rearrange("p (j x q) -> p j x q", j=4, x=2)[:, :, side, :]
            return copy(attn_T[side * QT:(side + 1) * QT, 4 * half:4 * half + 4, QT * tile:QT * (tile + 1)], src)

        def rot_table(turn, n, u):
            if isinstance(turn, int):
                return rot[:, turn % 2:turn % 2 + 1, n, u, :]
            return rot[:, bass.ds(turn % 2, 1), n, u, :]

        def v_chunk(nominal, u, s):
            ago, half = (1, 0) if s == 3 else (2, 1)
            if s % 2 and in_body(nominal, u, 0, SLOTS * ago):
                return ago, half
            return None, None

        def wqkv_piece(it, n):
            at = (it // BATCHES + 1) % 2 * (3 * INNER) + it % BATCHES * (2 * PIECE) + n * PIECE
            return slice(at, at + PIECE) if isinstance(it, int) else bass.ds(at, PIECE)

        def maximum_off(dve, b, lg, wide, rows32):
            dve.wait_ge(logits_biased, b + 1)
            dve.tensor_reduce(h_red[:, b, :], lg[b], AX, ALU.max).then_inc(logits_max_ready, 1)
            dve.wait_ge(logits_max_ready, b + 1)
            dve.tensor_tensor(lg[b], lg[b], wide(h_red[:, b, :], rows32), ALU.subtract).then_inc(logits_less_max, 1)

        block = ctx.enter_context(nc.Block())

        FF_LOADS = 16 * (1 + 3 * len(HID_PARTS) + 3)

        @block.sync
        def _(sp):
            sp.dma_start(const[:, :], consts[:, 0:C_BODY]).then_inc(const_in, 16)
            sp.dma_start(start_const, consts[:, C_BODY:C_END]).then_inc(start_const_in, 16)
            sp.dma_start(x_tok[:, :, :], x.rearrange("b (t p) c -> p (b t) c", p=P)).then_inc(x_in, 16)
            sp.dma_start(ctx_k[:, :, :], ctx_mem[:, :, 0:DIM].rearrange("b k c -> k b c")).then_inc(ctx_in, 16)
            for quad in range(4):
                sp.dma_start(ctx_v[quad * XKEYS:(quad + 1) * XKEYS, :, :],
                             ctx_mem[:, :, DIM:2 * DIM].rearrange("b k c -> k b c")).then_inc(ctx_in, 16)
            sp.dma_start(mask_i[:, :], mask.rearrange("(o b) k -> o (b k)", o=1).to_broadcast([P, BATCHES * XKEYS])
                         ).then_inc(small_in, 16)
            for dst, src in ((xbias[:, :], xb), (gates[:, 0:1], g_xattn), (gates[:, 1:2], g_ffn)):
                sp.dma_start(dst, src.rearrange("(o n) -> o n", o=1).to_broadcast([P, 1])).then_inc(small_in, 16)
            for n, src in enumerate((q_scale, k_scale)):
                s3 = src.rearrange("(o l) d -> o l d", o=1)
                sp.dma_start(head_scales[:, n, :, :], s3.to_broadcast([P, DEPTH, DHEAD])).then_inc(scales_in, 16)

            def load_pieces(row, first, count):
                for n in range(2):
                    if count > 0 or not isinstance(count, int):
                        sp.wait_ge(const_in, 16)
                        sp.wait_ge(wqkv_high_ready, count + n - 1)
                        sp.wait_ge(wqkv_low_ready, count + n - 1)
                    src = rows(wqkv, row, DIM)[:, (first + n) * PIECE:(first + n + 1) * PIECE]
                    sp.dma_start(wqkv_raw[:, n, :], src).then_inc(wqkv_in[n], 16)

            def rows(t, at, n):
                return t[at:at + n, :] if isinstance(at, int) else t[bass.ds(at, n), :]

            def load_wo(layer):
                sp.dma_start(wo_sb[:, :, :], rows(wo, layer * INNER, INNER).rearrange("(j p) c -> p j c", p=P)
                             ).then_inc(wo_in, 16)

            def load_ff(layer):
                sp.dma_start(w1_sb[:, :], rows(w1, layer * DIM, DIM)).then_inc(ff_w_in, 16)
                at = 0
                for j, m in enumerate(HID_PARTS):
                    sp.dma_start(w2_sb[0:m, j, :], rows(w2, layer * HIDDEN + at, m)).then_inc(ff_w_in, 16)
                    for part in range(2):
                        sp.dma_start(b1_sb[0:m, part, j:j + 1], rows(b1, layer * 2 * HIDDEN + part * HIDDEN + at, m)
                                     ).then_inc(ff_w_in, 16)
                    at += m
                for dst, src in ((ln_g_sb, ln_g), (ln_b_sb, ln_b), (b2_sb, b2)):
                    sp.dma_start(dst[:, :], rows(src, layer * DIM, DIM)).then_inc(ff_w_in, 16)

            load_wo(0)
            load_ff(0)
            for first in range(0, PIECES, 2):
                load_pieces(0, first, first)
            for first in range(0, PIECES, 2):
                load_pieces(DIM, first, PIECES + first)

            def next_layer(layer, wqkv_too):
                if wqkv_too:
                    load_pieces((layer + 1) * DIM, 0, PIECES * (layer + 1))
                sp.wait_ge(wo_ready, BATCHES * layer)
                load_wo(layer)
                if wqkv_too:
                    load_pieces((layer + 1) * DIM, 2, PIECES * (layer + 1) + 2)
                sp.wait_ge(w2_ready, BATCHES * layer)
                sp.wait_ge(stream_ready, BATCHES * layer)
                load_ff(layer)
                if wqkv_too:
                    for first in range(4, PIECES, 2):
                        load_pieces((layer + 1) * DIM, first, PIECES * (layer + 1) + first)

            with sp.Fori(1, DEPTH - 1) as layer:
                next_layer(layer, True)
            next_layer(DEPTH - 1, False)
            for b in range(BATCHES):
                sp.wait_ge(tail_dve, b + 1)
                sp.dma_start(out[b].rearrange("(t p) c -> p t c", p=P),
                             x_tok[:, b * BLOCKS:(b + 1) * BLOCKS, :]).then_inc(out_stored, 16)
            sp.wait_ge(out_stored, 16 * BATCHES)


        @block.gpsimd
        def _(pool):
            pool.memset(exps[:, :, :, 0:WINDOW], 0.0)
            pool.memset(probs[:, 1, :, 0:WINDOW], 0.0)
            pool.memset(minus_half[:, :], -0.5)
            pool.memset(mean_w[:, :], 1.0 / DIM)
            pool.memset(ln_eps[:, :], LN_EPS)
            pool.memset(shifted_high[:, 0, 0:WINDOW + 1].bitcast(F32), 0.0)
            pool.memset(shifted_low[:, 0, 0:WINDOW + 1].bitcast(F32), 0.0)
            pool.memset(ff_in[:, 0:1], 0.0).then_inc(setup_pool, 1)
            pool.wait_ge(scales_in, 16 * 2)
            pool.wait_ge(const_in, 16)

            def tables(turn):
                for n, at in enumerate((C_COS_Q, C_SIN_Q, C_COS_K, C_SIN_K)):
                    base = const[:, at:at + BLOCKS * DHEAD].rearrange("p (o u d) -> p o u d", o=1, d=DHEAD)
                    if isinstance(turn, int):
                        dst = rot[:, turn % 2:turn % 2 + 1, n, :, :]
                        scales = head_scales[:, n // 2, turn // BATCHES:turn // BATCHES + 1, :]
                    else:
                        dst = rot[:, bass.ds(turn % 2, 1), n, :, :]
                        scales = head_scales[:, n // 2, bass.ds(turn // BATCHES, 1), :]
                    scales = scales.rearrange("p o (u d) -> p o u d", u=1)
                    if n % 2 == 0:
                        last = pool.tensor_tensor(dst, base, scales.to_broadcast([P, 1, BLOCKS, DHEAD]), ALU.mult)
                        continue
                    for h in range(2):
                        here, other = slice(h * HALF, (h + 1) * HALF), slice((1 - h) * HALF, (2 - h) * HALF)
                        last = pool.tensor_tensor(dst[:, :, :, here], base[:, :, :, here],
                                                  scales[:, :, :, other].to_broadcast([P, 1, BLOCKS, HALF]), ALU.mult)
                last.then_inc(tables_ready, 1)

            tables(0)

            def split_low(piece, n, count):
                pool.wait_ge(wqkv_high_ready, count + 1)
                pool.tensor_tensor(wqkv_low[:, piece], wqkv_raw[:, n, :], wqkv_high[:, piece].bitcast(F32),
                                   ALU.subtract).then_inc(wqkv_low_ready, 1)

            for i in range(PIECES):
                split_low(slice(i * PIECE, (i + 1) * PIECE), i % 2, i)
            pool.wait_ge(stream_kept, BATCHES)
            pool.memset(k_T[:, :, 0:WINDOW], 0.0)
            pool.memset(q_diag[:, :, :, :, :], 0.0).then_inc(setup_pool, 1)

            def slot(it, nominal, u, s):
                K = PER_TURN * it + SLOTS * u + s
                if in_body(nominal, u, s, 3):
                    c, cs = K - 3, (s - 3) % SLOTS
                    pool.wait_ge(sin_ready, c + 1)
                    pool.wait_ge(cos_ready, c + 1)
                    pool.tensor_tensor(rotated[:, cs, :], rotated[:, cs, :], sin_part[:, cs % 2, :],
                                       ALU.add).then_inc(rotated_ready, 1)
                if in_body(nominal, u, s, 0):
                    pool.wait_ge(floored_ready, K + 1)
                    pool.tensor_tensor(inv_norm[:, s, :], norm2_floored[:, s, :], minus_half[:, :],
                                       ALU.pow).then_inc(inv_norm_ready, 1)
                n = {(2, 1): 0, (2, 3): 1}.get((u, s))
                if n is not None and nominal < TURNS - BATCHES:
                    split_low(wqkv_piece(it, n), n, PIECES + 2 * it + n)
                if s == 3 and u == 1 and nominal + 1 < TURNS:
                    pool.wait_ge(scales_in, 16 * 2)
                    pool.wait_ge(cos_ready, PER_TURN * it)
                    tables(it + 1)
                if in_body(nominal, u, s, 1):
                    c = K - 1
                    cs, cu, ct = (s - 1) % SLOTS, (u if s else (u - 1) % BLOCKS), (it if s or u else it - 1)
                    pool.wait_ge(scales_in, 16 * 2)
                    pool.wait_ge(normed_ready, c + 1)
                    after(pool, rotated_ready, c - 1)
                    pool.wait_ge(tables_ready, ct + 1)
                    src = normed[:, cs % 2, :].rearrange("p (h x d) -> p h x d", x=2, d=HALF)
                    dst = sin_part[:, cs % 2, :].rearrange("p (h x d) -> p h x d", x=2, d=HALF)
                    for h in range(2):
                        part = rot_table(ct, 1 if cs < 2 else 3, cu)[:, :, h * HALF:(h + 1) * HALF]
                        last = pool.tensor_tensor(dst[:, :, h, :], src[:, :, 1 - h, :],
                                                  part.to_broadcast([P, 8, HALF]), ALU.mult)
                    last.then_inc(sin_ready, 1)

            turns(pool, slot)

        @block.scalar
        def _(act):
            act.wait_ge(small_in, 16 * 4)
            act.activation(tanh_gates[:, :], gates[:, :], ACT.Tanh).then_inc(setup_dve, 1)
            act.wait_ge(setup_pool, 1)

            def split_high(piece, n, pair):
                act.wait_ge(wqkv_in[n], 16 * (pair + 1))
                act.copy(wqkv_high[:, piece], wqkv_raw[:, n, :]).then_inc(wqkv_high_ready, 1)


            def root(n):
                for b in range(BATCHES):
                    act.wait_ge(x_centred, BATCHES * n + b + 1)
                    act.activation(h_T[b], h_x[b], ACT.Square).then_inc(x_squared, 1)
                act.wait_ge(var_sums_ready, BATCHES * (n + 1))
                act.activation(h_stat[:, 3, :, :], h_stat[:, 2, :, :], ACT.Sqrt, bias=ln_eps[:, :],
                               scale=1.0 / DIM).then_inc(x_std_ready, 1)

            def split_pair(i):
                for n in range(2):
                    piece = 2 * i + n
                    split_high(slice(piece * PIECE, (piece + 1) * PIECE), n, i)

            root(0)
            split_pair(0)
            for b in range(BATCHES):
                act.wait_ge(xT_ready, b + 1)
                act.copy(h_T[b], ps[:, 2 * b, :].rearrange("p (a c) -> p a c", c=P)).then_inc(xT_kept, 1)
            split_pair(1)
            for b in range(BATCHES):
                act.wait_ge(logits_less_max, b + 1)
                act.activation(h_logit[b], h_logit[b], ACT.Exp).then_inc(x_exp_ready, 1)
            split_pair(2)
            for b in range(BATCHES):
                act.wait_ge(x_probsT_ready, b + 1)
                act.copy(h_expT[b], ps[:, 2 * b:2 * b + 2, :].rearrange("p a n -> p (a n)")).then_inc(x_probsT_kept, 1)
            split_pair(3)
            root(1)
            for b in range(BATCHES):
                act.wait_ge(streamT_ready, b + 1)
                act.copy(stream[:, b, :], ps[:, 2 * b + 1, :]).then_inc(stream_kept, 1)

            def split_next(n, it):
                act.wait_ge(scales_in, 16 * 2)
                after(act, v_ready, 2 * BLOCKS * it)
                split_high(wqkv_piece(it, n), n, PIECES // 2 + it)

            def slot(it, nominal, u, s):
                K = PER_TURN * it + SLOTS * u + s
                if in_body(nominal, u, s, 10):
                    G = K - 10
                    act.wait_ge(pT_ready, G + 1)
                    after(act, o_ready, G - 1)
                    act.copy(probs_T[:, s % 2, :, :],
                             ps[:, PS_PT, :].rearrange("p (j q) -> p j q", j=4)).then_inc(pT_kept, 1)
                t = ff_turn(it, nominal, 2)
                if t is not None and (u, s) == (0, 3):
                    act.wait_ge(gate_kept, 3 * t + 3)
                    act.activation(gate_sb[:, :, :], gate_sb[:, :, :], ACT.Gelu).then_inc(gelu_ready, 1)
                if (u, s) == (2, 0) and nominal < TURNS - BATCHES:
                    split_next(0, it)
                if in_body(nominal, u, s, 5):
                    c, cs, cu = K - 5, (s - 1) % SLOTS, (SLOTS * u + s - 5) // SLOTS % BLOCKS
                    act.wait_ge(qkT_ready, c + 1)
                    after(act, s_ready, c - cs - 4)
                    if cs == 0 and nominal <= 1:
                        act.wait_ge(setup_pool, 2)
                    if cs < 2:
                        keep_q(act.copy, 0, cs, cu).then_inc(q_top_ready, 1)
                    else:
                        j = cs - 2
                        act.copy(k_T[:, 4 * j:4 * j + 4, WINDOW + P * cu:WINDOW + P * (cu + 1)],
                                 ps[:, PS_QKT, :].rearrange("p (j t) -> p j t", j=4)).then_inc(k_ready, 1)
                if in_body(nominal, u, s, 11):
                    G = K - 11
                    act.wait_ge(o_ready, G + 1)
                    if is_first_group(u, s, 11):
                        after(act, wo_ready, it)
                    keep_o(act.copy, 0, u, s, 11).then_inc(o_top_kept, 1)
                if in_body(nominal, u, s, 0):
                    act.wait_ge(proj_ready, K + 1)
                    after(act, norm2_ready, K - 1)
                    act.activation(squares[:, s % 2, :], ps[:, s % 2, :], ACT.Square).then_inc(squares_ready, 1)
                if in_body(nominal, u, s, 8):
                    G = K - 8
                    act.wait_ge(neg_max_ready, G + 1)
                    after(act, probs_ready, G - 1)
                    for j in range(4):
                        last = act.activation(exps[:, s % 2, j, WINDOW:P], ps[:, PS_S, j * KT:(j + 1) * KT], ACT.Exp,
                                              bias=neg_max[:, s % 2, j:j + 1],
                                              accum_out=row_sum[:, s % 2, j:j + 1])
                    last.then_inc(exp_ready, 1)
                ago, half = v_chunk(nominal, u, s)
                if half is not None:
                    b = BLOCKS * it + u - ago
                    cols = slice(512 * half, 512 * half + 512)
                    act.wait_ge(v_ready, 2 * b + half + 1)
                    after(act, o_ready, SLOTS * (b - 2) + half + 3)
                    act.copy(v_last[:, (u - ago) % 2, cols], ps[:, PS_V, :]).then_inc(v_last_kept, 1)
                    after(act, o_ready, SLOTS * (b - 2) + half + 1)
                    act.copy(v_first[0:QT, (u - ago) % 2, cols], ps[0:QT, PS_V, :]).then_inc(v_first_kept, 1)
                if s % 2 == 0 and in_body(nominal, u, 0, SLOTS * 2):
                    b, half = BLOCKS * it + u - 2, s // 2
                    act.wait_ge(v_ready, 2 * b + half + 1)
                    after(act, o_ready, SLOTS * (b - 1) + half + 1)
                    act.copy(v_first[P - WINDOW:P, (u - 1) % 2, 512 * half:512 * half + 512],
                             ps[P - WINDOW:P, PS_V, :]).then_inc(v_before_kept, 1)
                if (u, s) == (2, 2) and nominal < TURNS - BATCHES:
                    split_next(1, it)
                t = ff_turn(it, nominal, 1)
                if t is not None and (u, s) == (2, 3):
                    act.wait_ge(centred, t + 1)
                    act.activation(ff_std[:, :], ff_in[:, :], ACT.Square).then_inc(ff_sq_ready, 1)
                if t is not None and (u, s) == (3, 0):
                    act.wait_ge(var_ready, t + 1)
                    after(act, ff_norm_ready, t)
                    act.activation(ff_std[:, :], ps[:, PS_FF, :], ACT.Sqrt, bias=ln_eps[:, :]).then_inc(std_ready, 1)

            turns(act, slot)

        @block.vector
        def _(dve):
            dve.wait_ge(const_in, 16)
            dve.wait_ge(start_const_in, 16)
            dve.tensor_copy(ident_bf[:, :], ident)
            dve.tensor_copy(band_bf[:, :, :], band.rearrange("p (a k) -> p a k", a=2))
            dve.memset(gate_sb[:, :, :], 0.0)
            dve.memset(v_first[QT:P, :, :], 0.0)
            dve.wait_ge(small_in, 16 * 4)
            bias = logit_bias[:, :, :].rearrange("p b k -> p (b k)")
            dve.tensor_copy(bias, mask_i[:, :]).then_inc(setup_dve, 1)
            dve.wait_ge(setup_dve, 2)
            dve.tensor_scalar(bias, bias, -1.0, 1e30, ALU.add, ALU.mult).then_inc(setup_dve, 1)
            dve.wait_ge(ctxT_ready, 1)
            head_of_row = head_of_channel.rearrange("p (h k) -> p h k", k=1)
            for b in range(BATCHES):
                dve.tensor_tensor(key_diag[:, b, :].rearrange("p (h k) -> p h k", h=XHEADS),
                                  ps[:, 0, b * XKEYS:(b + 1) * XKEYS].rearrange("p (h k) -> p h k", h=1)
                                  .to_broadcast([P, XHEADS, XKEYS]),
                                  head_of_row.to_broadcast([P, XHEADS, XKEYS]), ALU.mult)
            dve.wait_ge(ctx_in, 16 * 5)
            for b in range(BATCHES):
                dve.tensor_tensor(value_diag[:, 2 * b:2 * b + 2, :],
                                  ctx_v[:, b:b + 1, :].to_broadcast([P, 2, DIM]),
                                  head_of_key.rearrange("p (a c) -> p a c", a=2), ALU.mult)
            dve.wait_ge(setup_dve, 3)
            last = dve.tensor_scalar(bias, bias, xbias[:, 0:1], None, ALU.add)
            last.then_inc(setup_dve, 1)
            dve.wait_ge(setup_dve, 4)
            dve.wait_ge(x_in, 16)

            tiles = [x_tok[:, b * BLOCKS:(b + 1) * BLOCKS, :] for b in range(BATCHES)]
            rows32 = [P, BLOCKS * XHEADS, XKEYS]

            def wide(ap, shape):
                return ap.rearrange("p (a c) -> p a c", c=1).to_broadcast(shape)

            def layernorm(n):
                for b in range(BATCHES):
                    dve.tensor_reduce(h_stat[:, 0, b, :], tiles[b], AX, ALU.add).then_inc(sums_ready, 1)
                dve.wait_ge(sums_ready, BATCHES * (n + 1))
                dve.tensor_scalar(h_stat[:, 1, :, :], h_stat[:, 0, :, :], 1.0 / DIM, None, ALU.mult
                                  ).then_inc(means_ready, 1)
                dve.wait_ge(means_ready, n + 1)
                for b in range(BATCHES):
                    dve.tensor_tensor(h_x[b], tiles[b], wide(h_stat[:, 1, b, :], [P, BLOCKS, DIM]), ALU.subtract
                                      ).then_inc(x_centred, 1)
                for b in range(BATCHES):
                    dve.wait_ge(x_squared, BATCHES * n + b + 1)
                    dve.tensor_reduce(h_stat[:, 2, b, :], h_T[b], AX, ALU.add).then_inc(var_sums_ready, 1)
                dve.wait_ge(x_std_ready, n + 1)
                dve.reciprocal(h_stat[:, 4, :, :], h_stat[:, 3, :, :]).then_inc(x_inv_ready, 1)
                dve.wait_ge(x_inv_ready, n + 1)
                for b in range(BATCHES):
                    dve.tensor_tensor(h_x[b], h_x[b], wide(h_stat[:, 4, b, :], [P, BLOCKS, DIM]), ALU.mult
                                      ).then_inc(x_normed, 1)

            layernorm(0)
            lg = [h_logit[b].rearrange("p (m k) -> p m k", k=XKEYS) for b in range(BATCHES)]
            for b in range(BATCHES):
                dve.wait_ge(logits_ready, b + 1)
                logits = ps[:, 2 * b:2 * b + 2, :].rearrange("p a n -> p (a n)").rearrange("p (m k) -> p m k", k=XKEYS)
                dve.scalar_tensor_tensor(lg[b], logits, XSCALE, logit_bias[:, b:b + 1, :].to_broadcast(rows32),
                                         ALU.mult, ALU.add).then_inc(logits_biased, 1)
                if b > 0:
                    maximum_off(dve, b - 1, lg, wide, rows32)
            maximum_off(dve, BATCHES - 1, lg, wide, rows32)
            for b in range(BATCHES):
                dve.wait_ge(x_exp_ready, b + 1)
                dve.tensor_reduce(h_red[:, b, :], lg[b], AX, ALU.add).then_inc(exp_sums_ready, 1)
                if b % 2:
                    dve.wait_ge(exp_sums_ready, b + 1)
                    dve.reciprocal(h_inv[:, b - 1:b + 1, :], h_red[:, b - 1:b + 1, :]).then_inc(inv_sums_ready, 1)
                    dve.wait_ge(inv_sums_ready, (b + 1) // 2)
                    for i in (b - 1, b):
                        dve.tensor_tensor(lg[i], lg[i], wide(h_inv[:, i, :], rows32), ALU.mult
                                          ).then_inc(x_probs_ready, 1)
            for b in range(BATCHES):
                dve.wait_ge(attended_ready, b + 1)
                dve.scalar_tensor_tensor(tiles[b], ps[:, 2 * b, :].rearrange("p (a c) -> p a c", c=P),
                                         tanh_gates[:, 0:1], tiles[b], ALU.mult, ALU.add).then_inc(residual_ready, 1)
            dve.wait_ge(residual_ready, BATCHES)
            layernorm(1)
            dve.wait_ge(stream_kept, BATCHES)

            def shift(it, u, count):
                src = pick(stream, it % BATCHES)
                lo = P * u - (WINDOW if u else 0)
                first = 0 if u else 1
                parts = []
                for rows, late in ((slice(0, QT), 0), (slice(QT, P), 1)):
                    skip = first * late
                    at = WINDOW + P * u + skip - P * u if u == 0 else 0
                    parts.append((rows, slice(at, WINDOW + P), src[rows, lo + skip - late:P * (u + 1) - late]))
                for rows, to, block in parts:
                    last = dve.tensor_copy(shifted_high[rows, u, to], block)
                last.then_inc(high_ready, 1)
                dve.wait_ge(high_ready, count)
                for rows, to, block in parts:
                    last = dve.tensor_tensor(shifted_low[rows, u, to], block, shifted_high[rows, u, to].bitcast(F32),
                                             ALU.subtract)
                last.then_inc(shifted_ready, 1)

            shift(0, 0, 1)

            def slot(it, nominal, u, s):
                K = PER_TURN * it + SLOTS * u + s
                t1, t2 = ff_turn(it, nominal, 1), ff_turn(it, nominal, 2)
                if s == 0 and nominal * BLOCKS + u + 1 < TURNS * BLOCKS:
                    after(dve, v_ready, 2 * (BLOCKS * it + u - 2))
                    shift(it if u < 3 else it + 1, (u + 1) % BLOCKS, BLOCKS * it + u + 2)
                if t2 is not None and (u, s) == (0, 0):
                    dve.wait_ge(scaled_ready, t2 + 1)
                    dve.tensor_scalar(ff_in[:, :], ff_in[:, :], ln_b_sb[:, 0:1], None, ALU.add
                                      ).then_inc(ff_norm_ready, 1)
                if in_body(nominal, u, s, 8):
                    G = K - 8
                    dve.wait_ge(s_ready, G + 1)
                    scores = ps[:, PS_S, 0:4 * KT].rearrange("p (j k) -> p j k", j=4)
                    dve.tensor_reduce(neg_max[:, s % 2, :], scores, AX, ALU.max, negate=True).then_inc(neg_max_ready, 1)
                if in_body(nominal, u, s, 11):
                    G = K - 11
                    dve.wait_ge(o_ready, G + 1)
                    if is_first_group(u, s, 11):
                        after(dve, wo_ready, it)
                    keep_o(dve.tensor_copy, 1, u, s, 11).then_inc(o_low_kept, 1)
                if in_body(nominal, u, s, 2):
                    c, cs = K - 2, (s - 2) % SLOTS
                    cu, ct = (u if s > 1 else (u - 1) % BLOCKS), (it if s > 1 or u else it - 1)
                    dve.wait_ge(normed_ready, c + 1)
                    dve.wait_ge(tables_ready, ct + 1)
                    after(dve, qkT_ready, c - 3)
                    dve.tensor_tensor(rotated[:, cs, :].rearrange("p (h d) -> p h d", h=8),
                                      normed[:, cs % 2, :].rearrange("p (h d) -> p h d", h=8),
                                      rot_table(ct, 0 if cs < 2 else 2, cu).to_broadcast([P, 8, DHEAD]),
                                      ALU.mult).then_inc(cos_ready, 1)
                if t1 is not None and (u, s) == (3, 1):
                    invert_deviation(t1, 0)
                    invert_deviation(t1, 1)
                if t2 is not None and (u, s) == (0, 0):
                    gate(t2, 0)
                if t2 is not None and (u, s) == (0, 2):
                    gate(t2, 2)
                if t2 is not None and (u, s) == (0, 3):
                    hidden(t2, 0)
                if in_body(nominal, u, s, 1):
                    c, cs = K - 1, (s - 1) % SLOTS
                    dve.wait_ge(inv_norm_ready, c + 1)
                    after(dve, sin_ready, c - 1)
                    dve.tensor_tensor(normed[:, cs % 2, :].rearrange("p (h d) -> p h d", h=8),
                                      ps[:, cs % 2, :].rearrange("p (h d) -> p h d", h=8),
                                      inv_norm[:, cs, :].rearrange("p (h d) -> p h d", d=1)
                                      .to_broadcast([P, 8, DHEAD]), ALU.mult).then_inc(normed_ready, 1)
                if in_body(nominal, u, s, 0):
                    dve.wait_ge(squares_ready, K + 1)
                    dve.tensor_reduce(norm2[:, s, :], squares[:, s % 2, :].rearrange("p (h d) -> p h d", h=8), AX,
                                      ALU.add).then_inc(norm2_ready, 1)
                if t1 is not None and (u, s) == (2, 2):
                    dve.wait_ge(wo_ready, t1 + 1)
                    dve.tensor_tensor(mid[:, :], ps[:, PS_FF, :], pick(stream, t1 % BATCHES), ALU.add
                                      ).then_inc(mid_ready, 1)
                if t1 is not None and (u, s) == (2, 3):
                    dve.wait_ge(mean_ready, t1 + 1)
                    dve.tensor_tensor(ff_in[:, :], ff_in[:, :], ps[:, PS_FF, :], ALU.subtract).then_inc(centred, 1)
                if t1 is not None and (u, s) == (3, 1):
                    invert_deviation(t1, 2)
                if t2 is not None and (u, s) == (0, 3):
                    hidden(t2, 1)
                if in_body(nominal, u, s, 8):
                    G, r = K - 8, s % 2
                    dve.wait_ge(exp_ready, G + 1)
                    dve.reciprocal(inv_sum[:, r, :], row_sum[:, r, :]).then_inc(inv_sum_ready, 1)
                if in_body(nominal, u, s, 4) and s < 2:
                    c = K - 4
                    dve.wait_ge(qkT_ready, c + 1)
                    after(dve, s_ready, c - s - 4)
                    if s == 0 and nominal <= 1:
                        dve.wait_ge(setup_pool, 2)
                    keep_q(dve.tensor_copy, 1, s, (u - 1) % BLOCKS).then_inc(q_low_ready, 1)
                if t1 is not None and (u, s) == (2, 2):
                    dve.wait_ge(mid_ready, t1 + 1)
                    dve.tensor_copy(ff_in[0:QT, :], mid[0:QT, :])
                    dve.memset(ff_in[QT:P, 0:1], 0.0)
                    dve.tensor_copy(ff_in[QT:P, 1:TOKENS], mid[QT:P, 0:TOKENS - 1]).then_inc(ff_in_ready, 1)
                if t1 is not None and (u, s) == (3, 2):
                    invert_deviation(t1, 3)
                if t1 is not None and (u, s) == (3, 3):
                    dve.wait_ge(inv_std_ready, 4 * (t1 + 1))
                    dve.wait_ge(ff_w_in, FF_LOADS * (t1 // BATCHES + 1))
                    dve.scalar_tensor_tensor(ff_in[:, :], ff_in[:, :], ln_g_sb[:, 0:1], ff_std[:, :],
                                             ALU.mult, ALU.mult).then_inc(scaled_ready, 1)
                if in_body(nominal, u, s, 0):
                    dve.wait_ge(norm2_ready, K + 1)
                    dve.tensor_scalar(norm2_floored[:, s, :], norm2[:, s, :], NORM_FLOOR ** 2, None,
                                      ALU.max).then_inc(floored_ready, 1)
                if in_body(nominal, u, s, 8):
                    G, r = K - 8, s % 2
                    dve.wait_ge(inv_sum_ready, G + 1)
                    after(dve, pT_ready, G)
                    if s < 2:
                        out, shape = probs[:, 0, :, :].rearrange("p j (x k) -> p j x k", x=2)[:, :, ::-1, :], [P, 4, 2, QT]
                        source = exps[:, r, :, :].rearrange("p j (x k) -> p j x k", x=2)
                        inverse = inv_sum[:, r, :].rearrange("p (j x k) -> p j x k", x=1, k=1)
                    else:
                        out, source, shape = probs[:, 1, :, WINDOW:P], exps[:, r, :, WINDOW:P], [P, 4, KT]
                        inverse = inv_sum[:, r, :].rearrange("p (j k) -> p j k", k=1)
                    dve.tensor_tensor(out, source, inverse.to_broadcast(shape), ALU.mult).then_inc(probs_ready, 1)
                if t2 is not None and (u, s) == (0, 1):
                    gate(t2, 1)
                if (nominal, u, s) == (TURNS + 1, 0, 2):
                    for b in range(BATCHES - 1):
                        tail(b)
                if t2 is not None and (u, s) == (1, 3):
                    hidden(t2, 2)
                if t2 is not None and (u, s) == (2, 0):
                    dve.wait_ge(w2_ready, t2 + 1)
                    dve.scalar_tensor_tensor(pick(stream, t2 % BATCHES), ps[:, w2_bank(t2), :], b2_sb[:, 0:1], mid[:, :],
                                             ALU.add, ALU.add).then_inc(stream_ready, 1)

            def invert_deviation(t, part):
                dve.wait_ge(std_ready, t + 1)
                cols = slice(P * part, P * (part + 1))
                dve.reciprocal(ff_std[:, cols], ff_std[:, cols]).then_inc(inv_std_ready, 1)

            def gate(t, j):
                m = HID_PARTS[j]
                dve.wait_ge(gate_ready, 3 * t + j + 1)
                after(dve, w2_ready, t)
                dve.tensor_scalar(gate_sb[0:m, j, :], ps[0:m, gate_bank(t, j), :], b1_sb[0:m, 1, j:j + 1], None, ALU.add
                                  ).then_inc(gate_kept, 1)

            def hidden(t, j):
                m = HID_PARTS[j]
                dve.wait_ge(lin_ready, 3 * t + j + 1)
                dve.wait_ge(gelu_ready, t + 1)
                dve.scalar_tensor_tensor(gate_sb[0:m, j, :], ps[0:m, lin_bank(t, j), :], b1_sb[0:m, 0, j:j + 1],
                                         gate_sb[0:m, j, :], ALU.add, ALU.mult).then_inc(hidden_ready, 1)

            def tail(b):
                dve.wait_ge(tail_pe, b + 1)
                dve.scalar_tensor_tensor(tiles[b], ps[:, b, :].rearrange("p (t c) -> p t c", c=DIM),
                                         tanh_gates[:, 1:2], tiles[b], ALU.mult, ALU.add).then_inc(tail_dve, 1)

            turns(dve, slot)
            tail(BATCHES - 1)

        @block.tensor
        def _(pe):
            pe.wait_ge(const_in, 16)
            pe.wait_ge(ctx_in, 16 * 5)
            for b in range(BATCHES):
                last = nc.tensor.transpose(ps[:, 0, b * XKEYS:(b + 1) * XKEYS], ctx_k[:, b, :], ident[0:XKEYS, 0:XKEYS])
            last.then_inc(ctxT_ready, 1)
            pe.wait_ge(setup_dve, 4)

            def transposed(bank, src):
                for i in range(BLOCKS):
                    last = nc.tensor.transpose(ps[:, bank, i * P:(i + 1) * P], src[:, i, :], ident)
                return last

            for b in range(BATCHES):
                pe.wait_ge(x_normed, b + 1)
                transposed(2 * b, h_x[b]).then_inc(xT_ready, 1)
            for b in range(BATCHES):
                pe.wait_ge(xT_kept, b + 1)
                for i in range(BLOCKS):
                    last = nc.tensor.matmul(ps[:, 2 * b + i // 2, 256 * (i % 2):256 * (i % 2) + 256], h_T[b][:, i, :],
                                            key_diag[:, b, :], start=True, stop=True)
                last.then_inc(logits_ready, 1)
            for b in range(BATCHES):
                pe.wait_ge(x_probs_ready, b + 1)
                for i in range(2 * BLOCKS):
                    last = nc.tensor.transpose(ps[:, 2 * b + i // 4, P * (i % 4):P * (i % 4) + P],
                                               h_logit[b][:, P * i:P * (i + 1)], ident)
                last.then_inc(x_probsT_ready, 1)
            for b in range(BATCHES):
                pe.wait_ge(x_probsT_kept, b + 1)
                for i in range(BLOCKS):
                    for j in range(2):
                        last = nc.tensor.matmul(ps[:, 2 * b, P * i:P * (i + 1)],
                                                h_expT[b][:, P * (2 * i + j):P * (2 * i + j + 1)],
                                                value_diag[:, 2 * b + j, :], start=(j == 0), stop=(j == 1))
                last.then_inc(attended_ready, 1)
            for b in range(BATCHES):
                pe.wait_ge(x_normed, BATCHES + b + 1)
                transposed(2 * b + 1, h_x[b]).then_inc(streamT_ready, 1)

            pe.wait_ge(stream_kept, BATCHES)
            pe.wait_ge(setup_pool, 1)

            def slot(it, nominal, u, s):
                K = PER_TURN * it + SLOTS * u + s
                half = s % 2
                if in_body(nominal, u, s, 8):
                    G = K - 8
                    gu = (u - 2) % BLOCKS
                    pe.wait_ge(q_top_ready, 2 * (BLOCKS * it + u - 2) + half + 1)
                    pe.wait_ge(q_low_ready, 2 * (BLOCKS * it + u - 2) + half + 1)
                    pe.wait_ge(k_ready, 2 * (BLOCKS * it + u - 2) + half + 1)
                    after(pe, exp_ready, G)
                    first = 0 if gu == 0 and s < 2 else 1
                    nc.tensor.matmul(ps[:, PS_S, 0:4 * KT].rearrange("p (j k) -> p j k", j=4), ident_bf[:, :],
                                     band_bf[:, first:first + 1, :].to_broadcast([P, 4, KT]), start=True, stop=False,
                                     skip_group_check=True)
                    t0 = P * gu + QT * (s // 2)
                    for j in range(4):
                        pair = 4 * half + j
                        last = nc.tensor.matmul(ps[:, PS_S, j * KT:(j + 1) * KT], q_diag[:, gu % 2, s // 2, pair, :],
                                                k_T[:, pair, t0:t0 + KT], start=False, stop=(j == 3),
                                                skip_group_check=True)
                    last.then_inc(s_ready, 1)
                if in_body(nominal, u, s, 0):
                    pe.wait_ge(wqkv_high_ready, PIECES * (it // BATCHES + 1))
                    pe.wait_ge(wqkv_low_ready, PIECES * (it // BATCHES + 1))
                    pe.wait_ge(shifted_ready, BLOCKS * it + u + 1)
                    after(pe, normed_ready, K - 1)
                    project(ps[:, s % 2, :], u, slice(WINDOW, WINDOW + P), it, 512 * s).then_inc(proj_ready, 1)
                ago, half = v_chunk(nominal, u, s)
                if half is not None:
                    b = BLOCKS * it + u - ago
                    after(pe, v_before_kept, 2 * b + half)
                    project(ps[:, PS_V, :], (u - ago) % BLOCKS, slice(WINDOW, WINDOW + P), it if u >= ago else it - 1,
                            2 * INNER + 512 * half).then_inc(v_ready, 1)
                if in_body(nominal, u, s, 9):
                    G = K - 9
                    pe.wait_ge(probs_ready, G + 1)
                    after(pe, pT_kept, G)
                    for j in range(4):
                        last = nc.tensor.transpose(ps[:, PS_PT, P * j:P * (j + 1)], probs[:, (s - 1) % SLOTS // 2, j, :], ident)
                    last.then_inc(pT_ready, 1)
                feed_forward(it, nominal, u, s)
                if (nominal, u, s) == (TURNS, 3, 1):
                    for b in range(BATCHES - 1):
                        tail(b)
                if in_body(nominal, u, s, 4):
                    c = K - 4
                    pe.wait_ge(rotated_ready, c + 1)
                    blocks_before = BLOCKS * it + u - 1
                    if s < 3:
                        after(pe, q_top_ready, 2 * blocks_before + min(s, 2))
                        after(pe, q_low_ready, 2 * blocks_before + min(s, 2))
                    after(pe, k_ready, 2 * blocks_before + max(s - 2, 0))
                    for j in range(4):
                        last = nc.tensor.transpose(ps[:, PS_QKT, P * j:P * (j + 1)],
                                                   rotated[:, s, P * j:P * (j + 1)], ident)
                    last.then_inc(qkT_ready, 1)
                if in_body(nominal, u, s, 10):
                    G = K - 10
                    g = (SLOTS * u + s - 10) % PER_TURN
                    pe.wait_ge(pT_kept, G + 1)
                    after(pe, o_top_kept, G)
                    after(pe, o_low_kept, G)
                    if s >= 2:
                        pe.wait_ge(v_first_kept, 2 * (BLOCKS * it + u - 2) + s % 2 + 1)
                        after(pe, v_before_kept, 2 * (BLOCKS * it + u - 3) + s % 2 + 1)
                        values = v_first[:, u % 2, :]
                    else:
                        pe.wait_ge(v_last_kept, 2 * (BLOCKS * it + u - 3) + s % 2 + 1)
                        values = v_last[:, (u - 3) % 2, :]
                    for j in range(4):
                        pair = 4 * (g % 2) + j
                        last = nc.tensor.matmul(ps[:, PS_O, P * j:P * (j + 1)], values[:, P * pair:P * (pair + 1)],
                                                probs_T[:, s % 2, j, :], start=True, stop=True)
                    last.then_inc(o_ready, 1)

            def project(out, u, tokens, it, at):
                for n, (x_part, w_part) in enumerate(((shifted_low, wqkv_high), (shifted_high, wqkv_low),
                                                      (shifted_high, wqkv_high))):
                    col = it // BATCHES % 2 * (3 * INNER) + at
                    w = w_part[:, col:col + 512] if isinstance(it, int) else w_part[:, bass.ds(col, 512)]
                    last = nc.tensor.matmul(out, x_part[:, u, tokens], w, start=(n == 0), stop=(n == 2))
                return last

            def feed_forward(it, nominal, u, s):
                bank = ps[:, PS_FF, :]
                t = ff_turn(it, nominal, 1)
                if t is not None and (u, s) in ((2, 1), (2, 2)):
                    part = s - 1
                    if part == 0:
                        pe.wait_ge(wo_in, 16 * (t // BATCHES + 1))
                        after(pe, stream_ready, t)
                    pe.wait_ge(o_top_kept, PER_TURN * t + 15 + part)
                    pe.wait_ge(o_low_kept, PER_TURN * t + 15 + part)
                    for j in range(4 * part, 4 * part + 4):
                        last = nc.tensor.matmul(bank, wo_sb[:, j, :], attn_T[:, j, :], start=(j == 0),
                                                stop=(j == PAIRS - 1))
                    if part == 1:
                        last.then_inc(wo_ready, 1)
                if t is not None and (u, s) == (2, 3):
                    pe.wait_ge(ff_in_ready, t + 1)
                    nc.tensor.matmul(bank, mean_w[:, :], ff_in[:, :], start=True, stop=True).then_inc(mean_ready, 1)
                if t is not None and (u, s) == (3, 0):
                    pe.wait_ge(ff_sq_ready, t + 1)
                    nc.tensor.matmul(bank, mean_w[:, :], ff_std[:, :], start=True, stop=True).then_inc(var_ready, 1)
                t = ff_turn(it, nominal, 2)
                if t is None:
                    return
                if u == 0 and s < 3:
                    gate(t, s)
                if (u, s) == (0, 3):
                    lin(t, 0)
                    lin(t, 1)
                if (u, s) == (1, 0):
                    lin(t, 2)
                if (u, s) == (2, 0):
                    pe.wait_ge(hidden_ready, 3 * t + 3)
                    for j, m in enumerate(HID_PARTS):
                        last = nc.tensor.matmul(ps[:, w2_bank(t), :], w2_sb[0:m, j, :], gate_sb[0:m, j, :],
                                                start=(j == 0), stop=(j == 2))
                    last.then_inc(w2_ready, 1)

            def gate(t, j):
                count = 3 * t + j
                hidden_part(t, j, HIDDEN, gate_kept, 3 * t if ends(t) else count, gate_bank(t, j), gate_ready)

            def lin(t, j):
                if ends(t):
                    hidden_part(t, j, 0, gate_kept, 3 * t + j, lin_bank(t, j), lin_ready)
                elif j == 0:
                    hidden_part(t, j, 0, gate_kept, 3 * t + 3, PS_FF, lin_ready)
                else:
                    hidden_part(t, j, 0, hidden_ready, 3 * t + j, PS_FF, lin_ready)

            def hidden_part(t, j, col, left, count, bank, ready):
                m, col = HID_PARTS[j], col + sum(HID_PARTS[:j])
                pe.wait_ge(ff_norm_ready, t + 1)
                pe.wait_ge(ff_w_in, FF_LOADS * (t // BATCHES + 1))
                after(pe, left, count)
                nc.tensor.matmul(ps[0:m, bank, :], w1_sb[:, col:col + m], ff_in[:, :], start=True, stop=True
                                 ).then_inc(ready, 1)

            def tail(b):
                pe.wait_ge(stream_ready, TURNS - BATCHES + b + 1)
                for i in range(BLOCKS):
                    last = nc.tensor.transpose(ps[:, b, i * P:(i + 1) * P], stream[:, b, i * P:(i + 1) * P], ident)
                last.then_inc(tail_pe, 1)

            turns(pe, slot)
            tail(BATCHES - 1)


_INS = ['x', 'ctx_2048', 'mask_BxS2_ik0', 'g_xattn', 'g_ffn', 'L0_xattn_b', 'L0_ffn_Wqkv', 'L0_ffn_q_scale',
        'L0_ffn_k_scale', 'L0_ffn_Wo', 'L0_ffn_ln_g', 'L0_ffn_ln_b', 'L0_ffn_W1', 'L0_ffn_b1', 'L0_ffn_W2',
        'L0_ffn_b2']
_SHAPES = {'L0_ffn_Wqkv': (DEPTH * DIM, 3 * INNER), 'L0_ffn_Wo': (DEPTH * INNER, DIM),
           'L0_ffn_W1': (DEPTH * DIM, 2 * HIDDEN), 'L0_ffn_W2': (DEPTH * HIDDEN, DIM),
           'L0_ffn_ln_g': (DEPTH * DIM, 1), 'L0_ffn_ln_b': (DEPTH * DIM, 1), 'L0_ffn_b2': (DEPTH * DIM, 1),
           'L0_ffn_b1': (DEPTH * 2 * HIDDEN, 1)}


def kernel(**inputs):
    import numpy as _np
    import concourse.bacc as _bacc
    from concourse import mybir as _mybir
    from concourse.bass_utils import run_bass_kernel_spmd as _run

    nc = _bacc.Bacc("TRN2", target_bir_lowering=False, num_devices=1)
    arrays, args = {}, []
    for name in _INS:
        a = _np.ascontiguousarray(inputs[name])
        a = a.reshape(_SHAPES.get(name, a.shape))
        arrays[f"in_{name}_dram"] = a
        args.append(nc.dram_tensor(f"in_{name}_dram", a.shape, _mybir.dt.from_np(a.dtype), kind="ExternalInput").ap())
    arrays["consts_dram"] = shape_constants()
    args.append(nc.dram_tensor("consts_dram", (P, C_END), F32, kind="ExternalInput").ap())
    args.append(nc.dram_tensor("out_dram", (BATCHES, TOKENS, DIM), F32, kind="ExternalOutput").ap())
    build(nc, *args)
    r = _run(nc, [arrays], core_ids=[0])
    return r.results[0]["out_dram"]
```
